# Optimizing a Trainium2 kernel written in Bass

```python
import numpy as np
import jax
import jax.numpy as jnp

def _softmax(x, axis=-1):
    return jax.nn.softmax(x, axis=axis)

def _gelu(x):
    return jax.nn.gelu(x, approximate=True)

def _silu(x):
    return jax.nn.silu(x)

def _sigmoid(x):
    return jax.nn.sigmoid(x)

def _layernorm(x, axis=-1, eps=1e-05):
    m = jnp.mean(x, axis=axis, keepdims=True)
    v = jnp.var(x, axis=axis, keepdims=True)
    return (x - m) / jnp.sqrt(v + eps)

def _scatter_add(tgt, idx, src, axis=0):
    return tgt.at[idx].add(src)

def _segment_sum(src, seg, n):
    return jax.ops.segment_sum(src, seg, n)
kernel_name = 'mk_adj_resnorm_d4_adj_r2_9febed'

def setup_inputs(seed: int=0):
    np.random.seed(seed)
    _w = jnp.asarray

    def _rec_inputs():
        import jax
        import jax.numpy as jnp
        _gk = jax.random.key(seed)
        x = -0.0003929 + 0.9999 * jax.random.normal(jax.random.fold_in(_gk, 1), (128, 128, 256), jnp.float32)
        _a = jax.random.bernoulli(jax.random.fold_in(_gk, 2), 0.125, (128, 128, 128))
        _a = jnp.logical_or(_a, jnp.swapaxes(_a, -1, -2))
        _a = jnp.logical_or(_a, jnp.eye(128, dtype=bool))
        _af = _a.astype(jnp.float32)
        _af = _af * jax.random.uniform(jax.random.fold_in(_gk, 3), (128, 128, 128), jnp.float32, 0.05, 1)
        adj = _af
        _nm = jnp.ones((128, 128), dtype=bool)
        nodemask = jnp.where(_nm, 1.0, 0.0).astype(jnp.float32)
        return (x, adj, nodemask)
    x, adj, nodemask = _rec_inputs()

    def _L0_gnn_setup():
        import jax, jax.numpy as jnp
        import numpy as np
        B, N, C_IN, C_OUT = (8, 2048, 256, 256)
        key = jax.random.key(seed)
        k1, k2, k3, k4 = jax.random.split(key, 4)
        node_features = jax.random.normal(k1, (B, N, C_IN), dtype=jnp.float32)
        adj_matrix = jax.random.uniform(k2, (B, N, N), dtype=jnp.float32)
        W = jax.random.normal(k3, (C_IN, C_OUT), dtype=jnp.float32) / np.sqrt(C_IN)
        b = jax.random.normal(k4, (C_OUT,), dtype=jnp.float32) * 0.01
        return {'node_features': node_features, 'adj_matrix': adj_matrix, 'W': W, 'b': b}
    _L0_gnn_all = _L0_gnn_setup()
    _L0_gnn_in = {k: v for k, v in _L0_gnn_all.items() if k in ('W', 'b')}
    del _L0_gnn_all

    def _L1_gnn_setup():
        import jax, jax.numpy as jnp
        import numpy as np
        B, N, IN_DIM, ATT_DIM = (2, 4096, 256, 256)
        key = jax.random.key(seed)
        k1, k2, k3, k4 = jax.random.split(key, 4)
        X = jax.random.normal(k1, (B, N, IN_DIM), dtype=jnp.float32)
        adj = jax.random.uniform(k2, (B, N, N), dtype=jnp.float32)
        mask = jnp.ones((B, N), dtype=jnp.float32)
        Wqk = jax.random.normal(k3, (IN_DIM, 2 * ATT_DIM), dtype=jnp.float32) / np.sqrt(IN_DIM)
        Wv = jax.random.normal(k4, (IN_DIM, IN_DIM), dtype=jnp.float32) / np.sqrt(IN_DIM)
        return {'X': X, 'adj': adj, 'mask': mask, 'Wqk': Wqk, 'Wv': Wv}
    _L1_gnn_all = _L1_gnn_setup()
    _L1_gnn_in = {k: v for k, v in _L1_gnn_all.items() if k in ('Wqk', 'Wv')}
    del _L1_gnn_all

    def _L2_gnn_setup():
        import jax, jax.numpy as jnp
        import numpy as np
        EMBED_DIM = 256
        NUM_HEADS = 8
        HEAD_DIM = EMBED_DIM // NUM_HEADS
        SCALE = HEAD_DIM ** (-0.5)
        B, S = (16, 512)
        key = jax.random.key(seed)
        ks = jax.random.split(key, 12)
        init = lambda k, shape: jax.random.normal(k, shape, dtype=jnp.float32) * EMBED_DIM ** (-0.5)
        return {'x': jax.random.normal(ks[0], (B, S, EMBED_DIM), dtype=jnp.float32), 'adj_matrix': jax.random.uniform(ks[1], (B, S, S), dtype=jnp.float32), 'bond_matrix': jax.random.uniform(ks[2], (B, S, S), dtype=jnp.float32), 'Wq': init(ks[3], (EMBED_DIM, EMBED_DIM)), 'bq': jnp.zeros((EMBED_DIM,), jnp.float32), 'Wk': init(ks[4], (EMBED_DIM, EMBED_DIM)), 'bk': jnp.zeros((EMBED_DIM,), jnp.float32), 'Wv': init(ks[5], (EMBED_DIM, EMBED_DIM)), 'bv': jnp.zeros((EMBED_DIM,), jnp.float32), 'Wo': init(ks[6], (EMBED_DIM, EMBED_DIM)), 'bo': jnp.zeros((EMBED_DIM,), jnp.float32), 'seq_len': S}
    _L2_gnn_all = _L2_gnn_setup()
    _L2_gnn_in = {k: v for k, v in _L2_gnn_all.items() if k in ('Wq', 'bq', 'Wk', 'bk', 'Wv', 'bv', 'Wo', 'bo')}
    del _L2_gnn_all

    def _L3_gnn_setup():
        import jax, jax.numpy as jnp
        import numpy as np
        EPS_LN = 1e-05

        def hypergraph_conv(x, adj, W, b):
            N, C, _ = adj.shape
            H = (adj != 0).astype(x.dtype)
            w = adj.reshape(N, -1)[:, :C]
            xw = jnp.einsum('ncd,hd->nch', x, W)
            Dn = jnp.einsum('nce,ne->nc', H, w)
            Dn = jnp.where(Dn > 0, 1.0 / Dn, 0.0)
            Be = H.sum(axis=1)
            Be = jnp.where(Be > 0, 1.0 / Be, 0.0)
            m = Be[:, :, None] * jnp.einsum('nce,nch->neh', H, xw)
            out = Dn[:, :, None] * jnp.einsum('nce,neh->nch', H, m)
            return out + b

        def layer_norm(x, g, b):
            mu = jnp.mean(x, axis=-1, keepdims=True)
            var = jnp.var(x, axis=-1, keepdims=True)
            return (x - mu) * jax.lax.rsqrt(var + EPS_LN) * g + b
        key = jax.random.key(seed)
        ks = jax.random.split(key, 4)
        N, C, Din, Dh, Dout = (16, 512, 256, 512, 256)
        x = jax.random.normal(ks[0], (N, C, Din), dtype=jnp.float32)
        adj = jax.random.uniform(ks[1], (N, C, C), dtype=jnp.float32, minval=0.1, maxval=1.0)
        W1 = jax.random.normal(ks[2], (Dh, Din), dtype=jnp.float32) * (1.0 / np.sqrt(Din))
        b1 = jnp.zeros((Dh,), dtype=jnp.float32)
        gamma = jnp.ones((Dh,), dtype=jnp.float32)
        beta = jnp.zeros((Dh,), dtype=jnp.float32)
        W2 = jax.random.normal(ks[3], (Dout, Dh), dtype=jnp.float32) * (1.0 / np.sqrt(Dh))
        b2 = jnp.zeros((Dout,), dtype=jnp.float32)
        return {'x': x, 'adj': adj, 'W1': W1, 'b1': b1, 'gamma': gamma, 'beta': beta, 'W2': W2, 'b2': b2}
    _L3_gnn_all = _L3_gnn_setup()
    _L3_gnn_in = {k: v for k, v in _L3_gnn_all.items() if k in ('W1', 'b1', 'gamma', 'beta', 'W2', 'b2')}
    del _L3_gnn_all
    return {'x': x, 'adj': adj, 'nodemask': nodemask, 'L0_gnn_W': _L0_gnn_in['W'], 'L0_gnn_b': _L0_gnn_in['b'], 'L1_gnn_Wqk': _L1_gnn_in['Wqk'], 'L1_gnn_Wv': _L1_gnn_in['Wv'], 'L2_gnn_Wq': _L2_gnn_in['Wq'], 'L2_gnn_bq': _L2_gnn_in['bq'], 'L2_gnn_Wk': _L2_gnn_in['Wk'], 'L2_gnn_bk': _L2_gnn_in['bk'], 'L2_gnn_Wv': _L2_gnn_in['Wv'], 'L2_gnn_bv': _L2_gnn_in['bv'], 'L2_gnn_Wo': _L2_gnn_in['Wo'], 'L2_gnn_bo': _L2_gnn_in['bo'], 'L3_gnn_W1': _L3_gnn_in['W1'], 'L3_gnn_b1': _L3_gnn_in['b1'], 'L3_gnn_gamma': _L3_gnn_in['gamma'], 'L3_gnn_beta': _L3_gnn_in['beta'], 'L3_gnn_W2': _L3_gnn_in['W2'], 'L3_gnn_b2': _L3_gnn_in['b2']}

def reference(x, adj, nodemask, L0_gnn_W, L0_gnn_b, L1_gnn_Wqk, L1_gnn_Wv, L2_gnn_Wq, L2_gnn_bq, L2_gnn_Wk, L2_gnn_bk, L2_gnn_Wv, L2_gnn_bv, L2_gnn_Wo, L2_gnn_bo, L3_gnn_W1, L3_gnn_b1, L3_gnn_gamma, L3_gnn_beta, L3_gnn_W2, L3_gnn_b2):
    import jax
    import jax.numpy as jnp

    def _L0_gnn_ref(node_features, adj_matrix, W, b):
        import jax, jax.numpy as jnp
        import numpy as np
        B, N, C_IN, C_OUT = (8, 2048, 256, 256)
        num_neighbours = adj_matrix.sum(axis=-1, keepdims=True)
        h = jnp.einsum('bni,io->bno', node_features, W) + b
        h = jnp.einsum('bnm,bmo->bno', adj_matrix, h)
        return h / num_neighbours

    def _L1_gnn_ref(X, adj, mask, Wqk, Wv):
        import jax, jax.numpy as jnp
        import numpy as np
        B, N, IN_DIM, ATT_DIM = (2, 4096, 256, 256)
        qk = X @ Wqk
        q, k = jnp.split(qk, 2, axis=-1)
        v = X @ Wv
        att_dim = q.shape[-1]
        inv_scale = 1.0 / jnp.sqrt(jnp.float32(att_dim))
        k_m = k * mask[:, :, None]
        agg = jnp.einsum('bij,bjd->bid', adj, k_m)
        w = inv_scale * mask * jnp.einsum('bid,bid->bi', q, agg)
        L = jax.nn.softmax(w, axis=1)[:, :, None] * v
        return L

    def _L2_gnn_ref(x, adj_matrix, bond_matrix, Wq, bq, Wk, bk, Wv, bv, Wo, bo, seq_len):
        import jax, jax.numpy as jnp
        import numpy as np
        EMBED_DIM = 256
        NUM_HEADS = 8
        HEAD_DIM = EMBED_DIM // NUM_HEADS
        SCALE = HEAD_DIM ** (-0.5)
        B, S = (16, 512)
        b = x.shape[0]

        def proj(W, bias):
            y = jnp.einsum('bse,fe->bsf', x, W) + bias
            return y.reshape(b, seq_len, NUM_HEADS, HEAD_DIM).transpose(0, 2, 1, 3)
        q, k, v = (proj(Wq, bq), proj(Wk, bk), proj(Wv, bv))
        scores = jnp.einsum('bhqd,bhkd->bhqk', q, k) * SCALE
        mask = (adj_matrix + bond_matrix)[:, None, :, :]
        scores = scores * mask
        attn = jax.nn.softmax(scores, axis=-1)
        ctx = jnp.einsum('bhqk,bhkd->bhqd', attn, v)
        ctx = ctx.transpose(0, 2, 1, 3).reshape(b, seq_len, EMBED_DIM)
        return jnp.einsum('bse,fe->bsf', ctx, Wo) + bo

    def _L3_gnn_ref(x, adj, W1, b1, gamma, beta, W2, b2):
        import jax, jax.numpy as jnp
        import numpy as np
        EPS_LN = 1e-05

        def hypergraph_conv(x, adj, W, b):
            N, C, _ = adj.shape
            H = (adj != 0).astype(x.dtype)
            w = adj.reshape(N, -1)[:, :C]
            xw = jnp.einsum('ncd,hd->nch', x, W)
            Dn = jnp.einsum('nce,ne->nc', H, w)
            Dn = jnp.where(Dn > 0, 1.0 / Dn, 0.0)
            Be = H.sum(axis=1)
            Be = jnp.where(Be > 0, 1.0 / Be, 0.0)
            m = Be[:, :, None] * jnp.einsum('nce,nch->neh', H, xw)
            out = Dn[:, :, None] * jnp.einsum('nce,neh->nch', H, m)
            return out + b

        def layer_norm(x, g, b):
            mu = jnp.mean(x, axis=-1, keepdims=True)
            var = jnp.var(x, axis=-1, keepdims=True)
            return (x - mu) * jax.lax.rsqrt(var + EPS_LN) * g + b
        h = jax.nn.relu(hypergraph_conv(x, adj, W1, b1))
        h = layer_norm(h, gamma, beta)
        y = hypergraph_conv(h, adj, W2, b2)
        return y + x
    x = _layernorm(x + _L0_gnn_ref(x, adj, L0_gnn_W, L0_gnn_b), axis=-1)
    x = _layernorm(x + _L1_gnn_ref(x, adj, nodemask, L1_gnn_Wqk, L1_gnn_Wv), axis=-1)
    x = _layernorm(x + _L2_gnn_ref(x, adj, adj, L2_gnn_Wq, L2_gnn_bq, L2_gnn_Wk, L2_gnn_bk, L2_gnn_Wv, L2_gnn_bv, L2_gnn_Wo, L2_gnn_bo, 128), axis=-1)
    x = _layernorm(x + _L3_gnn_ref(x, adj, L3_gnn_W1, L3_gnn_b1, L3_gnn_gamma, L3_gnn_beta, L3_gnn_W2, L3_gnn_b2), axis=-1)
    return x

_drawn_inputs = setup_inputs


def setup_inputs(seed=0):
    import zlib

    import numpy as np

    out = dict(_drawn_inputs(seed))
    spreads = {'L2_gnn_bq': (0.0, 0.1),
     'L2_gnn_bk': (0.0, 0.8),
     'L2_gnn_bv': (0.0, 0.1),
     'L2_gnn_bo': (0.0, 0.1),
     'L3_gnn_b1': (0.0, 0.1),
     'L3_gnn_gamma': (1.0, 0.2),
     'L3_gnn_beta': (0.0, 0.1),
     'L3_gnn_b2': (0.0, 0.632)}
    factors = {}
    for name, (base, spread) in spreads.items():
        noise = np.random.default_rng([zlib.crc32(name.encode()), seed]).standard_normal(out[name].shape)
        drawn = base * np.exp(spread * noise) if base else spread * noise
        out[name] = jnp.asarray(drawn.astype(out[name].dtype))
    for name, factor in factors.items():
        out[name] = (out[name] * factor).astype(out[name].dtype)
    return out
```

```python
from contextlib import ExitStack

import concourse.bass as bass
from concourse import mybir

P = 128
G = 4
HEADS = 8
RG = 4
EPS = 1e-5
TINY = 1e-37

F32 = mybir.dt.float32
ALU = mybir.AluOpType
ACT = mybir.ActivationFunctionType
AX = mybir.AxisListType

FRONT = {"at", "ax", "h0", "ln0_stats", "ln0_aggr", "ln0_eps", "ln0_norm", "x1t", "amx", "xg",
         "wt", "pb", "v1", "ln1_stats", "ln1_aggr", "ln1_eps", "ln1_norm", "hold_a"}
BANKS = {"at": 1, "ax": 1, "h0": 1, "x1t": 1, "amx": 1, "xg": 1, "wt": 1, "pb": 1, "v1": 1,
         "x2t": 1, "q0": 1, "q1": 1, "k0": 1, "k1": 1, "v2": 1, "mp": 1, "sc": 4, "pt": 2,
         "cx": 1, "wo": 1, "tx": 1, "h1": 1, "mn": 1, "y": 1}


def lagged(steps, graphs=G):
    last = max(lag for _, lag in steps)
    return [[(s, k - lag) for s, lag in steps if 0 <= k - lag < graphs] for k in range(graphs + last)]


def layer_norm(name, lag):
    return [(f"{name}_stats", lag), (f"{name}_aggr", lag), (f"{name}_eps", lag),
            (f"{name}_norm", lag + 1)]


def front_slots():
    a = lagged([("at", 0), ("ax", 1), ("h0", 2)] + layer_norm("ln0", 2) + [("x1t", 4), ("amx", 4), ("xg", 4)])
    b = [[("wt", 0)], [("pb", 0)]]
    c = lagged([("v1", 0)] + layer_norm("ln1", 0))
    return a + b + c


def back_slots():
    a = [[("hyper", 0)]]
    a += lagged([("x2t", 0)])
    a += [[("q0", 0), ("q1", 0)], [("k0", 0), ("k1", 0)]]
    a += lagged([("mp", 0), ("v2", 0)])
    b = lagged([("sc", 0), ("attn", 0), ("attn2", 1), ("pt", 2), ("cx", 2), ("wo", 3)] + layer_norm("ln2", 3))
    b.append([("hold_a", 0)])
    c = lagged([("tx", 0), ("h1", 1)] + layer_norm("ln3", 1) + [("mn", 3), ("y", 4)] + layer_norm("ln4", 4))
    return a + b + c


def interleave(one, other):
    out, done = [], 0
    for n, slot in enumerate(one):
        out += slot
        want = (n + 1) * len(other) // len(one)
        for s in other[done:want]:
            out += s
        done = want
    return out


def flat(slots):
    return [s for slot in slots for s in slot]


BACK = back_slots()
SCHEDULE = interleave(BACK, front_slots())
SCHEDULE_FIRST = flat(front_slots()) + [("hold_a", 0)]
SCHEDULE_LAST = [s for s in flat(BACK) if s[0] != "hold_a"]


def place_banks(schedule):
    first, owner, order, at = {}, {}, [], 0
    for s in schedule:
        n = BANKS.get(s[0], 0)
        if not n:
            continue
        if at + n > 8:
            at = 0
        first[s] = at
        order.append((s, range(at, at + n)))
        at = (at + n) % 8
    before = {}
    for wrapped in (True, False):
        for s, banks in order:
            if not wrapped:
                before[s] = [owner[b] for b in banks if b in owner]
            for b in banks:
                owner[b] = (s, wrapped)
    return first, before


def build(nc, ins, out):
    x_d, adj_d = ins["x"], ins["adj"]
    B, N, D = x_d.shape
    D2 = ins["L3_gnn_W1"].shape[0]
    NG = B // G
    C, C2 = D // P, D2 // P
    assert N == P and B == P and C == 2
    HD = D // HEADS
    HC = 2.0 * HD ** -0.5
    INV = float(D) ** -0.5

    with ExitStack() as ctx:
        def sb(name, *shape):
            return ctx.enter_context(nc.sbuf_tensor(name, [P, *shape], F32))

        def sem(name):
            return ctx.enter_context(nc.semaphore(name))

        ps = ctx.enter_context(nc.psum_tensor("ps", [P, 8, 512], F32))

        ident, ones = sb("ident", P), sb("ones", P)
        w0, wv1, gram = sb("w0", C, D), sb("wv1", C, D), sb("gram", C, D)
        wqT, wkT, wvT, woT = (sb(n, C, D) for n in ("wqT", "wkT", "wvT", "woT"))
        w1T, w2T = sb("w1T", C, D2), sb("w2T", C2, D)
        b0_all, c2_all, b2_all, bw_all, b1_all = (sb(n, m) for n, m in (
            ("b0_all", D), ("c2_all", D), ("b2_all", D), ("bw_all", D), ("b1_all", D2)))
        bq_col, bk_col, maskT = sb("bq_col", C), sb("bk_col", C), sb("maskT", B)
        minus_half = sb("minus_half", 1)

        x_in, a_in = sb("x_in", G, D), sb("a_in", G, P)
        aT, amT, a_hold = sb("aT", G, P), sb("amT", G, P), sb("a_hold", G, P)
        mask, a_sum, a_rsum = sb("mask", G), sb("a_sum", G), sb("a_rsum", G)
        xb, axT, r0, x1 = sb("xb", G, D), sb("axT", 2, C, P), sb("r0", G, D), sb("x1", G, D)
        x1T, amx, junk = sb("x1T", G, C, P), sb("amx", 2, D), sb("junk", 2, D)
        w, wm, p_row, p_col = sb("w", G), sb("wm", G), sb("p_row", P), sb("p_col", G)
        e_row, w_stat = sb("e_row", P), sb("w_stat", 4)
        r1, x2 = sb("r1", G, D), sb("x2", G, D)
        hT, hb, mp = sb("hT", G, P), sb("hb", G, P + 2), sb("mp", G, P + 2)
        e_cnt, e_max, e_rcp = sb("e_cnt", G), sb("e_max", G), sb("e_rcp", G)
        d_max, d_rcp, d_inv, d_cnt = (sb(n, G) for n in ("d_max", "d_rcp", "d_inv", "d_cnt"))
        x2T, x2c = sb("x2T", C, G * P), sb("x2c", G, D)
        qT, kT, v2 = sb("qT", C, G * P), sb("kT", C, G * P), sb("v2", G, D)
        z = sb("z", 2, HEADS, P)
        z_max, z_sum, z_rcp = sb("z_max", 2, HEADS), sb("z_sum", 2, HEADS), sb("z_rcp", 2, HEADS)
        pT, cT = sb("pT", 2, HEADS, P), sb("cT", 2, C, P)
        r2, x3, x3b, x3c = sb("r2", G, D), sb("x3", G, D), sb("x3b", G, D), sb("x3c", G, D)
        txT, h1, hr, hn, mnT = sb("txT", 2, C, P), sb("h1", 2, D2), sb("hr", 3, D2), sb("hn", G, D2), sb("mnT", 2, C2, P)
        r3, y_out = sb("r3", G, D), sb("y_out", G, D)
        LNS = ("ln0", "ln1", "ln2", "ln3", "ln4")
        st = {n: sb(f"{n}_st", G, 6) for n in LNS}
        mv = {n: sb(f"{n}_mv", G, 2) for n in LNS}
        ve = {n: sb(f"{n}_ve", G) for n in LNS}
        rs = {n: sb(f"{n}_rs", G) for n in LNS}

        made = {s: sem(f"{s}_made") for s in BANKS}
        read = {s: sem(f"{s}_read") for s in BANKS}
        x_loaded, a_loaded = sem("x_loaded"), sem("a_loaded")
        mask_made, amT_made, a_summed, a_rsum_made, a_held = (sem(n) for n in (
            "mask_made", "amT_made", "a_summed", "a_rsum_made", "a_held"))
        xb_made, wm_made, p_max_made, p_bias_made, p_exp_made, p_rcp_made, p_row_made = (sem(n) for n in (
            "xb_made", "wm_made", "p_max_made", "p_bias_made", "p_exp_made", "p_rcp_made", "p_row_made"))
        hT_made, cnt_made, emax_made, ercp_made, hb_made = (sem(n) for n in (
            "hT_made", "cnt_made", "emax_made", "ercp_made", "hb_made"))
        d_step, d_made, x3c_made = sem("d_step"), sem("d_made"), sem("x3c_made")
        x2c_made, x3b_half, x3b_made = sem("x2c_made"), sem("x3b_half"), sem("x3b_made")
        max_made, sub_made, exp_made, sum_made, rcp_made, probs_made = (sem(n) for n in (
            "max_made", "sub_made", "exp_made", "sum_made", "rcp_made", "probs_made"))
        relu_made = sem("relu_made")
        stats_made, aggr_made, eps_made, root_made, norm_made = (
            {n: sem(f"{n}_{k}") for n in LNS} for k in ("stats", "aggr", "eps", "root", "norm"))
        out_stored = [sem(f"out_stored{g}") for g in range(G)]
        set_loaded, set_made, set_read, set_ready, set_ident = (sem(n) for n in (
            "set_loaded", "set_made", "set_read", "set_ready", "set_ident"))
        raw = {n: sb(f"raw_{n}", C, m) for n, m in (("qk1", 2 * D), ("q", D), ("k", D), ("v", D), ("o", D), ("w2", D2))}
        raw["w1"] = sb("raw_w1", C2, D)
        raw_mask, w2T_raw = sb("raw_mask", N), sb("w2T_raw", C2, D)
        wq1T, wk1T = sb("wq1T", C, D), sb("wk1T", C, D)
        bv_col, gamma_col, beta_col = sb("bv_col", C), sb("gamma_col", C2), sb("beta_col", C2)
        bo_all, bv_rep, beta_rep = sb("bo_all", D), sb("bv_rep", C, P), sb("beta_rep", C2, P)

        def nth(q, g):
            return q * G + (g + 1)

        def earlier(q, g, depth):
            return q * G + (g - depth + 1) if g >= depth else q * G

        def after(eng, semaphore, value):
            if not isinstance(value, int) or value > 0:
                eng.wait_ge(semaphore, value)

        def group_of(stage, it):
            return it + 1 if stage in FRONT else it

        per_group = {"wt", "pb", "q0", "q1", "k0", "k1"}

        def turned(name, rows, cols):
            return lambda r: [raw[name][:, c, r * P:(r + 1) * P] for c in range(cols)]

        TURNS = []
        for r in range(C):
            TURNS.append((wq1T[:, r, :], turned("qk1", C, C)(r)))
            TURNS.append((wk1T[:, r, :], turned("qk1", C, C)(C + r)))
            for n, t in (("q", wqT), ("k", wkT), ("v", wvT), ("o", woT)):
                TURNS.append((t[:, r, :], turned(n, C, C)(r)))
            TURNS.append((w1T[:, r, :], turned("w1", C, C2)(r)))
        for r in range(C2):
            TURNS.append((w2T_raw[:, r, :], turned("w2", C2, C)(r)))
        TURNS.append((maskT[:, :], [raw_mask[:, :]]))
        NT = len(TURNS)

        SET_LOADS = [
            (w0[:, :, :], ins["L0_gnn_W"].rearrange("(c p) n -> p c n", p=P)),
            (raw["qk1"][:, :, :], ins["L1_gnn_Wqk"].rearrange("(c p) n -> p c n", p=P)),
            (wv1[:, :, :], ins["L1_gnn_Wv"].rearrange("(c p) n -> p c n", p=P)),
            (raw["q"][:, :, :], ins["L2_gnn_Wq"].rearrange("(c p) n -> p c n", p=P)),
            (raw["k"][:, :, :], ins["L2_gnn_Wk"].rearrange("(c p) n -> p c n", p=P)),
            (raw["v"][:, :, :], ins["L2_gnn_Wv"].rearrange("(c p) n -> p c n", p=P)),
            (raw["o"][:, :, :], ins["L2_gnn_Wo"].rearrange("(c p) n -> p c n", p=P)),
            (raw["w1"][:, :, :], ins["L3_gnn_W1"].rearrange("(c p) n -> p c n", p=P)),
            (raw["w2"][:, :, :], ins["L3_gnn_W2"].rearrange("(c p) n -> p c n", p=P)),
            (raw_mask[:, :], ins["nodemask"]),
        ]
        for t, n in ((b0_all, "L0_gnn_b"), (bo_all, "L2_gnn_bo"), (b1_all, "L3_gnn_b1"), (b2_all, "L3_gnn_b2")):
            SET_LOADS.append((t[:, :], ins[n].unsqueeze(0).to_broadcast([P, ins[n].shape[0]])))
        for t, n in ((bq_col, "L2_gnn_bq"), (bk_col, "L2_gnn_bk"), (bv_col, "L2_gnn_bv"),
                     (gamma_col, "L3_gnn_gamma"), (beta_col, "L3_gnn_beta")):
            SET_LOADS.append((t[:, :], ins[n].rearrange("(c p) -> p c", p=P)))

        block = ctx.enter_context(nc.Block())

        @block.sync
        def _(sp):
            def load_x(q):
                after(sp, made["ax"], q * G)
                after(sp, xb_made, q * G)
                sp.dma_start(x_in[:, :, :], x_d[bass.ds(q * G, G)].rearrange("g n d -> n g d")).then_inc(x_loaded, 16)

            def load_a(q):
                after(sp, made["at"], q * G)
                after(sp, a_summed, q)
                after(sp, a_held, q)
                sp.dma_start(a_in[:, :, :], adj_d[bass.ds(q * G, G)].rearrange("g n m -> n g m")).then_inc(a_loaded, 16)

            def store(q):
                for g in range(G):
                    sp.wait_ge(norm_made["ln4"], nth(q, g))
                    sp.dma_start(out[bass.ds(q * G + g, 1)].rearrange("g n d -> n (g d)"),
                                 y_out[:, g, :]).then_inc(out_stored[g], 16)

            load_x(0)
            load_a(0)
            with nc.allow_non_contiguous_dma(reason="vectors, once"):
                for dst, src in SET_LOADS:
                    sp.dma_start(dst, src).then_inc(set_loaded, 16)
            load_x(1)
            load_a(1)
            with sp.Fori(0, NG - 2) as it:
                load_x(it + 2)
                load_a(it + 2)
                store(it)
            store(NG - 2)
            store(NG - 1)
            for g in range(G):
                sp.wait_ge(out_stored[g], 16 * NG)

        @block.tensor
        def _(pe):
            def bank(first, s):
                return ps[:, first[s], :]

            def ax(q, g, o):
                if g == 0:
                    pe.wait_ge(x_loaded, q * 16 + 16)
                pe.wait_ge(read["at"], nth(q, g))
                for c in range(C):
                    m = pe.matmul(o[:, c * P:(c + 1) * P], x_in[:, g, c * P:(c + 1) * P], aT[:, g, :], start=True, stop=True)
                return m

            def at(q, g, o):
                if g == 0:
                    pe.wait_ge(a_loaded, q * 16 + 16)
                return pe.transpose(o[:, 0:P], a_in[:, g, :], ident[:, :])

            def rows(o, left, right, chunks):
                for c in range(chunks):
                    m = pe.matmul(o, left(c), right(c), start=(c == 0), stop=(c == chunks - 1))
                return m

            def h0(q, g, o):
                pe.wait_ge(read["ax"], nth(q, g))
                return rows(o[:, 0:D], lambda c: axT[:, g % 2, c, :], lambda c: w0[:, c, :], C)

            def x1t(q, g, o):
                pe.wait_ge(norm_made["ln0"], nth(q, g))
                for c in range(C):
                    m = pe.transpose(o[:, c * P:(c + 1) * P], x1[:, g, c * P:(c + 1) * P], ident[:, :])
                return m

            def amx_(q, g, o):
                pe.wait_ge(amT_made, nth(q, g))
                return pe.matmul(o[:, 0:D], amT[:, g, :], x1[:, g, :], start=True, stop=True)

            def xg(q, g, o):
                pe.wait_ge(read["x1t"], nth(q, g))
                return rows(o[:, 0:D], lambda c: x1T[:, g, c, :], lambda c: gram[:, c, :], C)

            def wt(q, g, o):
                pe.wait_ge(wm_made, q + 1)
                return pe.transpose(o[0:G, 0:P], wm[:, :], ident[:, :])

            def pb(q, g, o):
                pe.wait_ge(p_row_made, q + 1)
                return pe.transpose(o[:, 0:P], p_row[:, :], ident[:, :])

            def v1(q, g, o):
                return rows(o[:, 0:D], lambda c: x1T[:, g, c, :], lambda c: wv1[:, c, :], C)

            def x2t(q, g, o):
                pe.wait_ge(norm_made["ln1"], nth(q, g))
                for c in range(C):
                    m = pe.transpose(o[:, c * P:(c + 1) * P], x2[:, g, c * P:(c + 1) * P], ident[:, :])
                return m

            def project(wT, f):
                def stage(q, g, o):
                    pe.wait_ge(read["x2t"], nth(q, G - 1))
                    return rows(o, lambda c: wT[:, c, f * P:(f + 1) * P], lambda c: x2T[:, c, :], C)
                return stage

            def v2_(q, g, o):
                pe.wait_ge(read["x2t"], nth(q, g))
                return rows(o[:, 0:D], lambda c: x2T[:, c, g * P:(g + 1) * P], lambda c: wvT[:, c, :], C)

            def mp_(q, g, o):
                pe.wait_ge(hb_made, nth(q, g))
                return pe.matmul(o[:, 0:P + 2], hT[:, g, :], hb[:, g, :], start=True, stop=True)

            def sc(q, g, o, b):
                if g == 0:
                    for s in ("q0", "q1", "k0", "k1"):
                        pe.wait_ge(read[s], q + 1)
                for r in range(RG):
                    for c in range(C):
                        at_ = slice(r * HD, (r + 1) * HD)
                        m = pe.matmul(ps[:, b + r, c * P:(c + 1) * P], qT[at_, c, g * P:(g + 1) * P],
                                      kT[at_, c, g * P:(g + 1) * P], start=True, stop=True)
                return m

            def pt(q, g, o, b):
                pe.wait_ge(probs_made, nth(q, g))
                for h in range(HEADS):
                    m = pe.transpose(ps[:, b + h // 4, (h % 4) * P:(h % 4 + 1) * P], z[:, g % 2, h, :], ident[:, :])
                return m

            def cx(q, g, o):
                pe.wait_ge(read["v2"], nth(q, g))
                pe.wait_ge(read["pt"], nth(q, g))
                for c in range(C):
                    for r in range(RG):
                        m = pe.matmul(o[r * HD:(r + 1) * HD, c * P:(c + 1) * P],
                                      v2[:, g, c * P + r * HD:c * P + (r + 1) * HD], pT[:, g % 2, r * C + c, :],
                                      start=True, stop=True)
                return m

            def wo(q, g, o):
                pe.wait_ge(read["cx"], nth(q, g))
                return rows(o[:, 0:D], lambda c: cT[:, g % 2, c, :], lambda c: woT[:, c, :], C)

            def tx(q, g, o):
                pe.wait_ge(norm_made["ln2"], nth(q, g))
                pe.wait_ge(read["mp"], nth(q, g))
                for c in range(C):
                    m = pe.matmul(o[:, c * P:(c + 1) * P], x3[:, g, c * P:(c + 1) * P], mp[:, g, 0:P], start=True, stop=True)
                return m

            def h1_(q, g, o):
                pe.wait_ge(read["tx"], nth(q, g))
                return rows(o, lambda c: txT[:, g % 2, c, :], lambda c: w1T[:, c, :], C)

            def mn(q, g, o):
                pe.wait_ge(norm_made["ln3"], nth(q, g))
                for c in range(C2):
                    m = pe.matmul(o[:, c * P:(c + 1) * P], hn[:, g, c * P:(c + 1) * P], mp[:, g, 0:P], start=True, stop=True)
                return m

            def y(q, g, o):
                pe.wait_ge(read["mn"], nth(q, g))
                return rows(o[:, 0:D], lambda c: mnT[:, g % 2, c, :], lambda c: w2T[:, c, :], C2)

            stages = {"at": at, "ax": ax, "h0": h0, "x1t": x1t, "amx": amx_, "xg": xg, "wt": wt, "pb": pb, "v1": v1,
                      "x2t": x2t, "q0": project(wqT, 0), "q1": project(wqT, 1), "k0": project(wkT, 0),
                      "k1": project(wkT, 1), "v2": v2_, "mp": mp_, "cx": cx, "wo": wo, "tx": tx, "h1": h1_,
                      "mn": mn, "y": y}
            wide = {"sc": sc, "pt": pt}

            def walk(schedule, it, again):
                first, before = place_banks(schedule)
                for s in schedule:
                    stage, g = s
                    if stage not in BANKS:
                        continue
                    need = {}
                    for (other, og), wrapped in before[s]:
                        if wrapped and not again:
                            continue
                        q = group_of(other, it)
                        if other in per_group:
                            v = (it if other not in FRONT else it + 1) if wrapped else q + 1
                        elif wrapped:
                            v = nth(it, og) if other in FRONT else it * G
                        else:
                            v = nth(q, og)
                        need.setdefault(other, []).append((og, wrapped, v))
                    for other, vs in need.items():
                        after(pe, read[other], max(vs, key=lambda t: (not t[1], t[0]))[2])
                    q, b = group_of(stage, it), first[s]
                    m = wide[stage](q, g, ps[:, b, :], b) if stage in wide else stages[stage](q, g, ps[:, b, :])
                    m.then_inc(made[stage], 1)

            pe.wait_ge(set_ident, 2)
            pe.wait_ge(set_loaded, 16 * len(SET_LOADS))
            for n, (_, blocks) in enumerate(TURNS):
                if n >= 8:
                    pe.wait_ge(set_read, n - 7)
                for k, blk in enumerate(blocks):
                    m = pe.transpose(ps[:, n % 8, k * P:(k + 1) * P], blk, ident[:, :])
                m.then_inc(set_made, 1)
            pe.wait_ge(set_read, NT)
            for r in range(C):
                rows(ps[:, r, 0:D], lambda c: wq1T[:, c, r * P:(r + 1) * P], lambda c: wk1T[:, c, :], C).then_inc(set_made, 1)
            pe.wait_ge(set_ready, C + C2)
            rows(ps[:, 2, 0:D], lambda c: bv_rep[:, c, :], lambda c: woT[:, c, :], C).then_inc(set_made, 1)
            rows(ps[:, 3, 0:D], lambda c: beta_rep[:, c, :], lambda c: w2T_raw[:, c, :], C2).then_inc(set_made, 1)
            pe.wait_ge(set_read, NT + 4)

            walk(SCHEDULE_FIRST, -1, False)
            for s in BANKS:
                if s in FRONT:
                    pe.wait_ge(read[s], 1 if s in per_group else G)
            walk(SCHEDULE, 0, True)
            with pe.Fori(1, NG - 1) as it:
                walk(SCHEDULE, it, True)
            for s in BANKS:
                k = NG if s in FRONT else NG - 1
                pe.wait_ge(read[s], k if s in per_group else k * G)
            walk(SCHEDULE_LAST, NG - 1, False)

        @block.scalar
        def _(act):
            def copy_out(stage, dst, shape=None, also=None):
                def run(q, g, o):
                    act.wait_ge(made[stage], q + 1 if stage in per_group else nth(q, g))
                    if also:
                        also(q, g)
                    d = dst(g)
                    src = o[:, 0:D] if shape is None else shape(o)
                    act.copy(d, src).then_inc(read[stage], 1)
                return run

            def pairs(o):
                return o[:, 0:C * P].rearrange("p (c n) -> p c n", c=C)

            def biased(stage, dst, bias):
                def run(q, g, o):
                    act.wait_ge(made[stage], q + 1)
                    after(act, made["sc"], q * G)
                    act.activation(dst, o, ACT.Identity, bias=bias).then_inc(read[stage], 1)
                return run

            def wt(q, g, o):
                act.wait_ge(p_bias_made, q + 1)
                act.activation(e_row[0:G, :], o[0:G, 0:P], ACT.Exp, bias=w_stat[0:G, 1:2], scale=INV,
                               accum_out=w_stat[0:G, 2:3]).then_inc(read["wt"], 1)

            def attn(q, g, o):
                act.wait_ge(sub_made, nth(q, g))
                act.activation(z[:, g % 2, :, :], z[:, g % 2, :, :], ACT.Exp, scale=HC).then_inc(exp_made, 1)

            def pt(q, g, o, b):
                act.wait_ge(made["pt"], nth(q, g))
                after(act, made["cx"], earlier(q, g, 2))
                act.copy(pT[:, g % 2, :, :].rearrange("p (b h) n -> p b (h n)", b=2), ps[:, b:b + 2, :]).then_inc(read["pt"], 1)

            def ln3_stats(q, g, o):
                act.wait_ge(read["h1"], nth(q, g))
                after(act, norm_made["ln3"], earlier(q, g, 3))
                act.activation(hr[:, g % 3, :], h1[:, g % 2, :], ACT.Relu).then_inc(relu_made, 1)

            stages = {
                "at": copy_out("at", lambda g: aT[:, g, :], lambda o: o[:, 0:P],
                               lambda q, g: after(act, hT_made, q)),
                "ax": copy_out("ax", lambda g: axT[:, g % 2, :, :], pairs,
                               lambda q, g: after(act, made["h0"], earlier(q, g, 2))),
                "x1t": copy_out("x1t", lambda g: x1T[:, g, :, :], pairs),
                "amx": copy_out("amx", lambda g: amx[:, g % 2, :], None,
                                lambda q, g: after(act, read["xg"], earlier(q, g, 2))),
                "wt": wt,
                "x2t": copy_out("x2t", lambda g: x2T[:, :, g * P:(g + 1) * P], pairs),
                "q0": biased("q0", qT[:, 0, :], bq_col[:, 0:1]), "q1": biased("q1", qT[:, 1, :], bq_col[:, 1:2]),
                "k0": biased("k0", kT[:, 0, :], bk_col[:, 0:1]), "k1": biased("k1", kT[:, 1, :], bk_col[:, 1:2]),
                "v2": copy_out("v2", lambda g: v2[:, g, :]),
                "mp": copy_out("mp", lambda g: mp[:, g, :], lambda o: o[:, 0:P + 2]),
                "attn": attn,
                "cx": copy_out("cx", lambda g: cT[:, g % 2, :, :], pairs,
                               lambda q, g: after(act, made["wo"], earlier(q, g, 2))),
                "tx": copy_out("tx", lambda g: txT[:, g % 2, :, :], pairs,
                               lambda q, g: after(act, made["h1"], earlier(q, g, 2))),
                "ln3_stats": ln3_stats,
                "mn": copy_out("mn", lambda g: mnT[:, g % 2, :, :], lambda o: o.rearrange("p (c n) -> p c n", c=C2),
                               lambda q, g: after(act, made["y"], earlier(q, g, 2))),
            }

            def walk(schedule, it):
                first, _ = place_banks(schedule)
                for s in schedule:
                    stage, g = s
                    q = group_of(stage, it)
                    if stage == "pt":
                        pt(q, g, None, first[s])
                    elif stage in stages:
                        stages[stage](q, g, ps[:, first[s], :] if s in first else None)

            walk(SCHEDULE_FIRST, -1)
            walk(SCHEDULE, 0)
            with act.Fori(1, NG - 1) as it:
                walk(SCHEDULE, it)
            walk(SCHEDULE_LAST, NG - 1)

        @block.gpsimd
        def _(pool):
            def root(n):
                def run(q, g):
                    pool.wait_ge(eps_made[n], nth(q, g))
                    pool.tensor_tensor(rs[n][:, g:g + 1], ve[n][:, g:g + 1], minus_half[:, :], ALU.pow).then_inc(root_made[n], 1)
                return run

            def at(q, g):
                if g == 0:
                    pool.wait_ge(x_loaded, q * 16 + 16)
                after(pool, read["h0"], q * G)
                pool.tensor_tensor(xb[:, g, :], x_in[:, g, :], b0_all[:, :], ALU.add).then_inc(xb_made, 1)

            def x2t(q, g):
                pool.wait_ge(norm_made["ln1"], nth(q, g))
                pool.tensor_tensor(x2c[:, g, :], x2[:, g, :], c2_all[:, :], ALU.add).then_inc(x2c_made, 1)

            def attn(q, g):
                zg = z[:, g % 2, :, :]
                pool.wait_ge(max_made, nth(q, g))
                pool.tensor_tensor(zg, zg, z_max[:, g % 2, :].unsqueeze(2).to_broadcast([P, HEADS, P]), ALU.subtract)\
                    .then_inc(sub_made, 1)

            def attn2(q, g):
                zg = z[:, g % 2, :, :]
                pool.wait_ge(rcp_made, nth(q, g))
                pool.tensor_tensor(zg, zg, z_rcp[:, g % 2, :].unsqueeze(2).to_broadcast([P, HEADS, P]), ALU.mult)\
                    .then_inc(probs_made, 1)

            def tx(q, g):
                pool.wait_ge(norm_made["ln2"], nth(q, g))
                after(pool, x3c_made, q * G)
                pool.tensor_tensor(x3b[:, g, :], x3[:, g, :], b2_all[:, :], ALU.add).then_inc(x3b_half, 1)
                pool.wait_ge(x3b_half, nth(q, g))
                pool.tensor_tensor(x3b[:, g, :], x3b[:, g, :], x3[:, g, :], ALU.add).then_inc(x3b_made, 1)

            stages = {"at": at, "x2t": x2t, "attn": attn, "attn2": attn2, "tx": tx}
            for n in ("ln0", "ln1", "ln2", "ln3", "ln4"):
                stages[f"{n}_eps"] = root(n)

            def walk(schedule, it):
                for stage, g in schedule:
                    if stage in stages:
                        stages[stage](group_of(stage, it), g)

            pool.memset(ones[:, :], 1.0).then_inc(set_ident, 1)
            pool.wait_ge(set_ident, 1)
            pool.affine_select(out=ident[:, :], in_=ones[:, :], compare_op=ALU.is_equal, fill=0.0, base=0,
                               pattern=[[-1, P]], channel_multiplier=1).then_inc(set_ident, 1)
            pool.wait_ge(set_loaded, 16 * len(SET_LOADS))
            pool.wait_ge(set_read, NT + 4)
            walk(SCHEDULE_FIRST, -1)
            walk(SCHEDULE, 0)
            with pool.Fori(1, NG - 1) as it:
                walk(SCHEDULE, it)
            walk(SCHEDULE_LAST, NG - 1)

        @block.vector
        def _(dve):
            def norm(n, src, width, dst, free):
                def stats(q, g):
                    if n == "ln3":
                        dve.wait_ge(relu_made, nth(q, g))
                    else:
                        dve.wait_ge(read[src_stage[n]], nth(q, g))
                    dve.bn_stats(st[n][:, g, :], src(g)).then_inc(stats_made[n], 1)

                def aggr(q, g):
                    dve.wait_ge(set_ident, 1)
                    dve.wait_ge(stats_made[n], nth(q, g))
                    dve.bn_aggr(mv[n][:, g, :], st[n][:, g, :]).then_inc(aggr_made[n], 1)

                def eps(q, g):
                    dve.wait_ge(aggr_made[n], nth(q, g))
                    dve.tensor_scalar(ve[n][:, g:g + 1], mv[n][:, g, 1:2], EPS, None, ALU.add).then_inc(eps_made[n], 1)

                def scale(q, g):
                    dve.wait_ge(root_made[n], nth(q, g))
                    free(q, g)
                    dve.tensor_scalar(dst(g), src(g), mv[n][:, g, 0:1], rs[n][:, g:g + 1],
                                      ALU.subtract, ALU.mult).then_inc(norm_made[n], 1)

                return {f"{n}_stats": stats, f"{n}_aggr": aggr, f"{n}_eps": eps, f"{n}_norm": scale}

            src_stage = {"ln0": "h0", "ln1": "v1", "ln2": "wo", "ln4": "y"}

            def at(q, g, o):
                if g == 0:
                    dve.wait_ge(a_loaded, q * 16 + 16)
                    after(dve, wm_made, q)
                    dve.tensor_copy(mask[:, :], maskT[:, bass.ds(q * G, G)]).then_inc(mask_made, 1)
                    dve.tensor_reduce(a_sum[:, :], a_in[:, :, :], AX.X, ALU.add).then_inc(a_summed, 1)
                    after(dve, read["h0"], q * G)
                    dve.wait_ge(a_summed, q + 1)
                    dve.reciprocal(a_rsum[:, :], a_sum[:, :]).then_inc(a_rsum_made, 1)
                    dve.wait_ge(mask_made, q + 1)

            def ax(q, g, o):
                dve.wait_ge(read["at"], nth(q, g))
                dve.wait_ge(mask_made, q + 1)
                dve.tensor_scalar(amT[:, g, :], aT[:, g, :], mask[:, g:g + 1], None, ALU.mult).then_inc(amT_made, 1)

            def h0(q, g, o):
                dve.wait_ge(made["h0"], nth(q, g))
                dve.wait_ge(xb_made, nth(q, g))
                dve.wait_ge(a_rsum_made, q + 1)
                dve.scalar_tensor_tensor(out=r0[:, g, :], in0=o[:, 0:D], scalar=a_rsum[:, g:g + 1], in1=xb[:, g, :],
                                         op0=ALU.mult, op1=ALU.add).then_inc(read["h0"], 1)

            def xg(q, g, o):
                dve.wait_ge(made["xg"], nth(q, g))
                dve.wait_ge(read["amx"], nth(q, g))
                dve.tensor_tensor_reduce(junk[:, g % 2, :], o[:, 0:D], amx[:, g % 2, :], 1.0, 0.0, ALU.mult, ALU.add,
                                         w[:, g:g + 1]).then_inc(read["xg"], 1)

            def wt(q, g, o):
                dve.wait_ge(read["xg"], nth(q, G - 1))
                dve.tensor_tensor(wm[:, :], w[:, :], mask[:, :], ALU.mult).then_inc(wm_made, 1)
                dve.wait_ge(made["wt"], q + 1)
                dve.tensor_reduce(w_stat[0:G, 0:1], o[0:G, 0:P], AX.X, ALU.max).then_inc(p_max_made, 1)
                dve.wait_ge(p_max_made, q + 1)
                dve.tensor_scalar(w_stat[0:G, 1:2], w_stat[0:G, 0:1], -INV, None, ALU.mult).then_inc(p_bias_made, 1)

            def pb(q, g, o):
                dve.wait_ge(read["wt"], q + 1)
                dve.reciprocal(w_stat[0:G, 3:4], w_stat[0:G, 2:3]).then_inc(p_rcp_made, 1)
                dve.wait_ge(p_rcp_made, q + 1)
                dve.tensor_scalar(p_row[0:G, :], e_row[0:G, :], w_stat[0:G, 3:4], None, ALU.mult).then_inc(p_row_made, 1)
                dve.wait_ge(made["pb"], q + 1)
                dve.tensor_copy(p_col[:, :], o[:, 0:G]).then_inc(read["pb"], 1)

            def v1(q, g, o):
                dve.wait_ge(made["v1"], nth(q, g))
                dve.wait_ge(read["pb"], q + 1)
                dve.scalar_tensor_tensor(out=r1[:, g, :], in0=o[:, 0:D], scalar=p_col[:, g:g + 1], in1=x1[:, g, :],
                                         op0=ALU.mult, op1=ALU.add).then_inc(read["v1"], 1)

            def hyper(q, g, o):
                after(dve, made["mp"], q * G)
                dve.tensor_copy(hb[:, :, P:P + 1], aT[:, :, 0:1]).then_inc(cnt_made, 1)
                dve.tensor_scalar(hT[:, :, :], aT[:, :, :], 0.0, None, ALU.not_equal).then_inc(hT_made, 1)
                dve.wait_ge(hT_made, q + 1)
                dve.tensor_reduce(e_cnt[:, :], hT[:, :, :], AX.X, ALU.add).then_inc(cnt_made, 1)
                dve.wait_ge(cnt_made, q * 2 + 2)
                dve.tensor_scalar(e_max[:, :], e_cnt[:, :], 1.0, None, ALU.max).then_inc(emax_made, 1)
                dve.wait_ge(emax_made, q + 1)
                dve.reciprocal(e_rcp[:, :], e_max[:, :]).then_inc(ercp_made, 1)
                dve.wait_ge(ercp_made, q + 1)
                for k in range(G):
                    dve.tensor_scalar(hb[:, k, 0:P], hT[:, k, :], e_rcp[:, k:k + 1], None, ALU.mult).then_inc(hb_made, 1)

            def mp_(q, g, o):
                dve.wait_ge(read["mp"], nth(q, g))
                after(dve, x3c_made, q * G)
                dsum = mp[:, g, P:P + 1]
                dve.tensor_scalar(d_max[:, g:g + 1], dsum, TINY, None, ALU.max).then_inc(d_step, 1)
                dve.wait_ge(d_step, q * (2 * G) + (2 * g + 1))
                dve.reciprocal(d_rcp[:, g:g + 1], d_max[:, g:g + 1]).then_inc(d_step, 1)
                dve.wait_ge(d_step, q * (2 * G) + (2 * g + 2))
                dve.scalar_tensor_tensor(out=d_inv[:, g:g + 1], in0=dsum, scalar=0.0, in1=d_rcp[:, g:g + 1],
                                         op0=ALU.is_gt, op1=ALU.mult).then_inc(d_made, 1)
                dve.wait_ge(d_made, q * (2 * G) + (2 * g + 1))
                dve.tensor_tensor(d_cnt[:, g:g + 1], d_inv[:, g:g + 1], mp[:, g, P + 1:P + 2], ALU.mult).then_inc(d_made, 1)

            def sc(q, g, o, b):
                dve.wait_ge(made["sc"], nth(q, g))
                dve.wait_ge(a_held, q + 1)
                after(dve, made["pt"], earlier(q, g, 2))
                zg = z[:, g % 2, :, :]
                for c in range(C):
                    m = dve.tensor_tensor(zg.rearrange("p (r c) n -> p r c n", c=C)[:, :, c, :],
                                          ps[:, b:b + RG, c * P:(c + 1) * P],
                                          a_hold[:, g, :].unsqueeze(1).to_broadcast([P, RG, P]), ALU.mult)
                m.then_inc(read["sc"], 1)
                dve.wait_ge(read["sc"], nth(q, g))
                dve.tensor_reduce(z_max[:, g % 2, :], zg, AX.X, ALU.max).then_inc(max_made, 1)

            def attn2(q, g, o):
                dve.wait_ge(exp_made, nth(q, g))
                dve.tensor_reduce(z_sum[:, g % 2, :], z[:, g % 2, :, :], AX.X, ALU.add).then_inc(sum_made, 1)
                dve.wait_ge(sum_made, nth(q, g))
                dve.reciprocal(z_rcp[:, g % 2, :], z_sum[:, g % 2, :]).then_inc(rcp_made, 1)

            def wo(q, g, o):
                dve.wait_ge(made["wo"], nth(q, g))
                dve.wait_ge(x2c_made, nth(q, g))
                dve.tensor_tensor(r2[:, g, :], o[:, 0:D], x2c[:, g, :], ALU.add).then_inc(read["wo"], 1)

            def h1_(q, g, o):
                dve.wait_ge(made["h1"], nth(q, g))
                dve.wait_ge(d_made, q * (2 * G) + 2 * G)
                after(dve, relu_made, earlier(q, g, 2))
                dve.scalar_tensor_tensor(out=h1[:, g % 2, :], in0=o, scalar=d_inv[:, g:g + 1], in1=b1_all[:, :],
                                         op0=ALU.mult, op1=ALU.add).then_inc(read["h1"], 1)

            def mn(q, g, o):
                dve.wait_ge(x3b_made, nth(q, g))
                after(dve, read["y"], q * G)
                dve.scalar_tensor_tensor(out=x3c[:, g, :], in0=bw_all[:, :], scalar=d_cnt[:, g:g + 1], in1=x3b[:, g, :],
                                         op0=ALU.mult, op1=ALU.add).then_inc(x3c_made, 1)

            def y(q, g, o):
                dve.wait_ge(made["y"], nth(q, g))
                dve.wait_ge(x3c_made, nth(q, g))
                dve.scalar_tensor_tensor(out=r3[:, g, :], in0=o[:, 0:D], scalar=d_inv[:, g:g + 1], in1=x3c[:, g, :],
                                         op0=ALU.mult, op1=ALU.add).then_inc(read["y"], 1)

            def hold_a(q, g, o):
                dve.wait_ge(a_loaded, q * 16 + 16)
                after(dve, read["sc"], q * G)
                dve.tensor_copy(a_hold[:, :, :], a_in[:, :, :]).then_inc(a_held, 1)

            def free1(q, g):
                after(dve, made["amx"], q * G)
                after(dve, read["v1"], q * G)

            def free2(q, g):
                after(dve, made["x2t"], q * G)
                after(dve, x2c_made, q * G)

            def free3(q, g):
                after(dve, made["tx"], q * G)
                after(dve, x3b_made, q * G)

            stages = {"at": at, "ax": ax, "h0": h0, "xg": xg, "wt": wt, "pb": pb, "v1": v1, "hyper": hyper, "mp": mp_,
                      "wo": wo, "h1": h1_, "mn": mn, "y": y, "hold_a": hold_a, "attn2": attn2}
            plain = {}
            plain.update(norm("ln0", lambda g: r0[:, g, :], D, lambda g: x1[:, g, :], free1))
            plain.update(norm("ln1", lambda g: r1[:, g, :], D, lambda g: x2[:, g, :], free2))
            plain.update(norm("ln2", lambda g: r2[:, g, :], D, lambda g: x3[:, g, :], free3))
            plain.update(norm("ln3", lambda g: hr[:, g % 3, :], D2, lambda g: hn[:, g, :],
                              lambda q, g: after(dve, made["mn"], q * G)))
            plain.update(norm("ln4", lambda g: r3[:, g, :], D, lambda g: y_out[:, g, :],
                              lambda q, g: after(dve, out_stored[g], q * 16)))

            def walk(schedule, it):
                first, _ = place_banks(schedule)
                for s in schedule:
                    stage, g = s
                    q = group_of(stage, it)
                    if stage == "sc":
                        sc(q, g, None, first[s])
                    elif stage in stages:
                        stages[stage](q, g, ps[:, first[s], :] if s in first else None)
                    elif stage in plain:
                        plain[stage](q, g)

            dve.memset(minus_half[:, :], -0.5)
            dve.memset(p_row[:, :], 0.0)
            dve.memset(hb[:, :, P + 1:P + 2], 1.0)
            dve.wait_ge(set_ident, 1)
            dve.wait_ge(set_loaded, 16 * len(SET_LOADS))
            for c in range(C):
                dve.tensor_scalar(bv_rep[:, c, :], ones[:, :], bv_col[:, c:c + 1], None, ALU.mult).then_inc(set_ready, 1)
            for c in range(C2):
                dve.tensor_scalar(beta_rep[:, c, :], ones[:, :], beta_col[:, c:c + 1], None, ALU.mult).then_inc(set_ready, 1)
            for n, (dst, blocks) in enumerate(TURNS):
                dve.wait_ge(set_made, n + 1)
                dve.tensor_copy(dst, ps[:, n % 8, 0:len(blocks) * P]).then_inc(set_read, 1)
            dve.wait_ge(set_read, NT)
            for c in range(C2):
                dve.tensor_scalar(w2T[:, c, :], w2T_raw[:, c, :], gamma_col[:, c:c + 1], None, ALU.mult)
            dve.wait_ge(set_made, NT + 4)
            dve.tensor_copy(gram[:, 0, :], ps[:, 0, 0:D]).then_inc(set_read, 1)
            dve.tensor_copy(gram[:, 1, :], ps[:, 1, 0:D]).then_inc(set_read, 1)
            dve.tensor_tensor(c2_all[:, :], ps[:, 2, 0:D], bo_all[:, :], ALU.add).then_inc(set_read, 1)
            dve.tensor_copy(bw_all[:, :], ps[:, 3, 0:D]).then_inc(set_read, 1)

            walk(SCHEDULE_FIRST, -1)
            walk(SCHEDULE, 0)
            with dve.Fori(1, NG - 1) as it:
                walk(SCHEDULE, it)
            walk(SCHEDULE_LAST, NG - 1)


_INS = ["x", "adj", "nodemask", "L0_gnn_W", "L0_gnn_b", "L1_gnn_Wqk", "L1_gnn_Wv", "L2_gnn_Wq", "L2_gnn_bq",
        "L2_gnn_Wk", "L2_gnn_bk", "L2_gnn_Wv", "L2_gnn_bv", "L2_gnn_Wo", "L2_gnn_bo", "L3_gnn_W1", "L3_gnn_b1",
        "L3_gnn_gamma", "L3_gnn_beta", "L3_gnn_W2", "L3_gnn_b2"]


def kernel(**inputs):
    import numpy as _np
    import concourse.bacc as _bacc
    from concourse import mybir as _mybir
    from concourse.bass_utils import run_bass_kernel_spmd as _run

    nc = _bacc.Bacc("TRN2", target_bir_lowering=False, num_devices=1)
    arrays, aps = {}, {}
    for name in _INS:
        a = _np.ascontiguousarray(inputs[name])
        arrays[f"in_{name}_dram"] = a
        aps[name] = nc.dram_tensor(f"in_{name}_dram", a.shape, _mybir.dt.from_np(a.dtype), kind="ExternalInput").ap()
    x = inputs["x"]
    out = nc.dram_tensor("out_0_dram", tuple(x.shape), _mybir.dt.from_np(_np.dtype(x.dtype)), kind="ExternalOutput").ap()
    build(nc, aps, out)
    r = _run(nc, [arrays], core_ids=[0])
    return r.results[0]["out_0_dram"]
```

```python
from contextlib import ExitStack

import concourse.bass as bass
from concourse import mybir

P = 128
G = 4
HEADS = 8
RG = 4
EPS = 1e-5
TINY = 1e-37

F32 = mybir.dt.float32
ALU = mybir.AluOpType
ACT = mybir.ActivationFunctionType
AX = mybir.AxisListType

FRONT = {"asum", "at", "am", "xb", "ax", "h0", "ln0_stats", "ln0_aggr", "ln0_root", "ln0_norm", "x1t", "amx", "xg", "wm", "wt", "wmax", "wexp",
         "wnorm", "pb", "pcol", "v1", "ln1_stats", "ln1_aggr", "ln1_root", "ln1_norm", "hold"}
BANKS = {"at": 1, "ax": 1, "h0": 1, "x1t": 1, "amx": 1, "xg": 1, "wt": 1, "pb": 1, "v1": 1,
         "x2t": 1, "q0": 1, "q1": 1, "k0": 1, "k1": 1, "v2": 1, "mp": 1, "sc": 4, "pt": 2,
         "cx": 1, "wo": 1, "tx": 1, "h1": 1, "mn": 1, "y": 1}


ORDER_TEXT = {
    "pe": """
        x2t.0 x2t.1 x2t.2 x2t.3 at.0 at.1 at.2 k0.0 q0.0 q1.0 k1.0 ax.0 sc.0 mp.0 ax.1 v2.0 at.3 sc.1 h0.0 mp.1
        ax.2 h0.1 ax.3 h0.2 sc.2 pt.0 v2.1 h0.3 amx.0 cx.0 pt.1 sc.3 mp.2 wo.0 v2.2 x1t.0 cx.1 mp.3 xg.0 x1t.1 v2.3
        wo.1 tx.0 xg.1 amx.1 pt.2 x1t.2 amx.2 h1.0 cx.2 pt.3 wo.2 x1t.3 tx.1 amx.3 cx.3 xg.2 wo.3 mn.0 h1.1 xg.3
        tx.2 v1.0 wt.0 h1.2 tx.3 v1.1 pb.0 h1.3 y.0 v1.2 mn.1 mn.2 v1.3 y.1 mn.3 y.2 y.3
    """,
    "act": """
        x2t.0 x2t.1 x2t.2 x2t.3 at.0 at.1 k0.0 q1.0 q0.0 at.2 k1.0 ax.0 v2.0 ax.1 at.3 mp.0 exp0.0 exp1.0 ax.2 mp.1
        ax.3 exp0.1 exp1.1 pt.0 v2.1 cx.0 exp0.2 amx.0 pt.1 exp1.2 x1t.0 mp.2 cx.1 exp1.3 v2.2 x1t.1 mp.3 exp0.3
        v2.3 tx.0 amx.1 x1t.2 amx.2 pt.2 cx.2 relu.0 pt.3 tx.1 x1t.3 cx.3 amx.3 mn.0 relu.1 tx.2 wexp.0 tx.3 relu.2
        relu.3 mn.1 mn.2 mn.3
    """,
    "dve": """
        hyper.0 asum.0 sc.0 am.0 zmax.0 sc.1 h0.0 zmax.1 zrcp.0 h0.1 ln0_stats.0 am.1 ln0_aggr.0 h0.2 ln0_stats.1
        ln0_stats.2 ln0_norm.0 zrcp.1 ln0_aggr.1 sc.2 am.2 ln0_aggr.2 zmax.2 h0.3 sc.3 wo.0 zmax.3 ln0_norm.1
        ln2_stats.0 ln2_aggr.0 xg.0 zrcp.2 am.3 ln2_norm.0 ln0_norm.2 wo.1 ln0_stats.3 zrcp.3 dinv.0 xg.1
        ln2_stats.1 ln2_aggr.1 ln0_aggr.3 h1.0 ln2_norm.1 ln0_norm.3 wo.2 ln3_stats.0 ln3_aggr.0 ln2_stats.2
        ln3_norm.0 wo.3 ln2_aggr.2 ln2_stats.3 ln2_aggr.3 xg.2 ln2_norm.2 h1.1 x3c.0 xg.3 wm.0 ln3_stats.1
        ln3_aggr.1 wmax.0 ln2_norm.3 wnorm.0 ln3_norm.1 h1.2 hold.0 x3c.1 pcol.0 v1.0 ln3_stats.2 ln3_aggr.2 h1.3
        ln1_stats.0 v1.1 ln1_aggr.0 y.0 ln3_norm.2 ln3_stats.3 ln4_stats.0 v1.2 ln3_aggr.3 ln1_stats.1 ln1_aggr.1
        ln4_aggr.0 v1.3 ln1_stats.2 ln3_norm.3 ln1_aggr.2 y.1 ln1_norm.0 ln1_stats.3 ln1_norm.1 ln1_norm.2
        ln4_stats.1 x3c.2 x3c.3 ln1_aggr.3 y.2 ln4_aggr.1 ln1_norm.3 ln4_stats.2 y.3 ln4_norm.0 ln4_stats.3
        ln4_norm.1 ln4_aggr.2 ln4_aggr.3 ln4_norm.2 ln4_norm.3
    """,
    "pool": """
        xb.0 xb.1 x2c.0 x2c.1 xb.2 x2c.2 xb.3 probs.0 ln0_root.0 x2c.3 probs.1 ln0_root.1 ln0_root.2 ln2_root.0
        probs.2 probs.3 ln0_root.3 ln2_root.1 ln3_root.0 ln2_root.2 x3b.0 ln2_root.3 ln3_root.1 x3b.1 x3b.2
        ln3_root.2 x3b.3 ln1_root.0 ln3_root.3 ln1_root.1 ln1_root.2 ln4_root.0 ln1_root.3 ln4_root.1 ln4_root.2
        ln4_root.3
    """,
}

def numbered(text):
    return [(word.split(".")[0], int(word.split(".")[1])) for word in text.split()]


ORDER = {engine: numbered(text) for engine, text in ORDER_TEXT.items()}
FIRST = {e: [s for s in order if s[0] in FRONT] for e, order in ORDER.items()}
LAST = {e: [s for s in order if s[0] not in FRONT] for e, order in ORDER.items()}


def place_banks(schedule):
    first, owner, order, at = {}, {}, [], 0
    for s in schedule:
        n = BANKS.get(s[0], 0)
        if not n:
            continue
        if at + n > 8:
            at = 0
        first[s] = at
        order.append((s, range(at, at + n)))
        at = (at + n) % 8
    before = {}
    for wrapped in (True, False):
        for s, banks in order:
            if not wrapped:
                before[s] = [owner[b] for b in banks if b in owner]
            for b in banks:
                owner[b] = (s, wrapped)
    return first, before


def build(nc, ins, out):
    x_d, adj_d = ins["x"], ins["adj"]
    B, N, D = x_d.shape
    D2 = ins["L3_gnn_W1"].shape[0]
    NG = B // G
    C, C2 = D // P, D2 // P
    assert N == P and B == P and C == 2
    HD = D // HEADS
    HC = 2.0 * HD ** -0.5
    INV = float(D) ** -0.5

    with ExitStack() as ctx:
        def sb(name, *shape):
            return ctx.enter_context(nc.sbuf_tensor(name, [P, *shape], F32))

        def sem(name):
            return ctx.enter_context(nc.semaphore(name))

        ps = ctx.enter_context(nc.psum_tensor("ps", [P, 8, 512], F32))

        ident, ones = sb("ident", P), sb("ones", P)
        w0, wv1, gram = sb("w0", C, D), sb("wv1", C, D), sb("gram", C, D)
        wqT, wkT, wvT, woT = (sb(n, C, D) for n in ("wqT", "wkT", "wvT", "woT"))
        w1T, w2T = sb("w1T", C, D2), sb("w2T", C2, D)
        b0_all, c2_all, b2_all, bw_all, b1_all = (sb(n, m) for n, m in (
            ("b0_all", D), ("c2_all", D), ("b2_all", D), ("bw_all", D), ("b1_all", D2)))
        bq_col, bk_col, maskT = sb("bq_col", C), sb("bk_col", C), sb("maskT", B)
        minus_half, eps_col = sb("minus_half", 1), sb("eps_col", 1)

        x_in, a_in = sb("x_in", G, D), sb("a_in", G, P)
        aT, amT, a_hold = sb("aT", G, P), sb("amT", G, P), sb("a_hold", G, P)
        mask, a_sum, a_rsum = sb("mask", G), sb("a_sum", G), sb("a_rsum", G)
        xb, axT, r0, x1 = sb("xb", G, D), sb("axT", 2, C, P), sb("r0", G, D), sb("x1", G, D)
        x1T, amx, junk = sb("x1T", G, C, P), sb("amx", 2, D), sb("junk", 2, D)
        w, wm, p_row, p_col = sb("w", G), sb("wm", G), sb("p_row", P), sb("p_col", G)
        e_row, w_stat = sb("e_row", P), sb("w_stat", 4)
        r1, x2 = sb("r1", G, D), sb("x2", G, D)
        hT, hb, mp = sb("hT", G, P), sb("hb", G, P + 2), sb("mp", G, P + 2)
        e_cnt, e_max, e_rcp = sb("e_cnt", G), sb("e_max", G), sb("e_rcp", G)
        d_max, d_rcp, d_inv, d_cnt = (sb(n, G) for n in ("d_max", "d_rcp", "d_inv", "d_cnt"))
        x2T, x2c = sb("x2T", C, G * P), sb("x2c", G, D)
        qT, kT, v2 = sb("qT", C, G * P), sb("kT", C, G * P), sb("v2", G, D)
        z = sb("z", 2, HEADS, P)
        z_max, z_sum, z_rcp = sb("z_max", 2, HEADS), sb("z_sum", 2, HEADS), sb("z_rcp", 2, HEADS)
        pT, cT = sb("pT", 2, HEADS, P), sb("cT", 2, C, P)
        r2, x3, x3b, x3c = sb("r2", G, D), sb("x3", G, D), sb("x3b", G, D), sb("x3c", G, D)
        txT, h1, hr, hn, mnT = sb("txT", 2, C, P), sb("h1", 2, D2), sb("hr", 3, D2), sb("hn", G, D2), sb("mnT", 2, C2, P)
        r3, y_out = sb("r3", G, D), sb("y_out", G, D)
        LNS = ("ln0", "ln1", "ln2", "ln3", "ln4")
        st = {n: sb(f"{n}_st", G, 6) for n in LNS}
        mv = {n: sb(f"{n}_mv", G, 2) for n in LNS}
        ve = {n: sb(f"{n}_ve", G) for n in LNS}
        rs = {n: sb(f"{n}_rs", G) for n in LNS}

        made = {s: sem(f"{s}_made") for s in BANKS}
        read = {s: sem(f"{s}_read") for s in BANKS}
        x_loaded, a_loaded = sem("x_loaded"), sem("a_loaded")
        mask_made, amT_made, a_summed, a_rsum_made, a_held = (sem(n) for n in (
            "mask_made", "amT_made", "a_summed", "a_rsum_made", "a_held"))
        xb_made, wm_made, p_max_made, p_bias_made, p_exp_made, p_rcp_made, p_row_made = (sem(n) for n in (
            "xb_made", "wm_made", "p_max_made", "p_bias_made", "p_exp_made", "p_rcp_made", "p_row_made"))
        hT_made, cnt_made, emax_made, ercp_made, hb_made = (sem(n) for n in (
            "hT_made", "cnt_made", "emax_made", "ercp_made", "hb_made"))
        d_step, d_made, x3c_made = sem("d_step"), sem("d_made"), sem("x3c_made")
        x2c_made, x3b_half, x3b_made = sem("x2c_made"), sem("x3b_half"), sem("x3b_made")
        max_made, exp0_made, exp1_made, rcp_made, probs_made = (sem(n) for n in (
            "max_made", "exp0_made", "exp1_made", "rcp_made", "probs_made"))
        relu_made = sem("relu_made")
        stats_made, aggr_made, eps_made, root_made, norm_made = (
            {n: sem(f"{n}_{k}") for n in LNS} for k in ("stats", "aggr", "eps", "root", "norm"))
        out_stored = [sem(f"out_stored{g}") for g in range(G)]
        set_loaded, set_made, set_read, set_ready, set_ident = (sem(n) for n in (
            "set_loaded", "set_made", "set_read", "set_ready", "set_ident"))
        raw = {n: sb(f"raw_{n}", C, m) for n, m in (("qk1", 2 * D), ("q", D), ("k", D), ("v", D), ("o", D), ("w2", D2))}
        raw["w1"] = sb("raw_w1", C2, D)
        raw_mask, w2T_raw = sb("raw_mask", N), sb("w2T_raw", C2, D)
        wq1T, wk1T = sb("wq1T", C, D), sb("wk1T", C, D)
        bv_col, gamma_col, beta_col = sb("bv_col", C), sb("gamma_col", C2), sb("beta_col", C2)
        bo_all, bv_rep, beta_rep = sb("bo_all", D), sb("bv_rep", C, P), sb("beta_rep", C2, P)

        def nth(q, g):
            return q * G + (g + 1)

        def earlier(q, g, depth):
            return q * G + (g - depth + 1) if g >= depth else q * G

        def after(eng, semaphore, value):
            if not isinstance(value, int) or value > 0:
                eng.wait_ge(semaphore, value)

        def group_of(stage, it):
            return it + 1 if stage in FRONT else it

        per_group = {"wt", "pb", "q0", "q1", "k0", "k1"}

        def turned(name, rows, cols):
            return lambda r: [raw[name][:, c, r * P:(r + 1) * P] for c in range(cols)]

        TURNS = []
        for r in range(C):
            TURNS.append((wq1T[:, r, :], turned("qk1", C, C)(r)))
            TURNS.append((wk1T[:, r, :], turned("qk1", C, C)(C + r)))
            for n, t in (("q", wqT), ("k", wkT), ("v", wvT), ("o", woT)):
                TURNS.append((t[:, r, :], turned(n, C, C)(r)))
            TURNS.append((w1T[:, r, :], turned("w1", C, C2)(r)))
        for r in range(C2):
            TURNS.append((w2T_raw[:, r, :], turned("w2", C2, C)(r)))
        TURNS.append((maskT[:, :], [raw_mask[:, :]]))
        NT = len(TURNS)

        SET_LOADS = [
            (w0[:, :, :], ins["L0_gnn_W"].rearrange("(c p) n -> p c n", p=P)),
            (raw["qk1"][:, :, :], ins["L1_gnn_Wqk"].rearrange("(c p) n -> p c n", p=P)),
            (wv1[:, :, :], ins["L1_gnn_Wv"].rearrange("(c p) n -> p c n", p=P)),
            (raw["q"][:, :, :], ins["L2_gnn_Wq"].rearrange("(c p) n -> p c n", p=P)),
            (raw["k"][:, :, :], ins["L2_gnn_Wk"].rearrange("(c p) n -> p c n", p=P)),
            (raw["v"][:, :, :], ins["L2_gnn_Wv"].rearrange("(c p) n -> p c n", p=P)),
            (raw["o"][:, :, :], ins["L2_gnn_Wo"].rearrange("(c p) n -> p c n", p=P)),
            (raw["w1"][:, :, :], ins["L3_gnn_W1"].rearrange("(c p) n -> p c n", p=P)),
            (raw["w2"][:, :, :], ins["L3_gnn_W2"].rearrange("(c p) n -> p c n", p=P)),
            (raw_mask[:, :], ins["nodemask"]),
        ]
        for t, n in ((b0_all, "L0_gnn_b"), (bo_all, "L2_gnn_bo"), (b1_all, "L3_gnn_b1"), (b2_all, "L3_gnn_b2")):
            SET_LOADS.append((t[:, :], ins[n].unsqueeze(0).to_broadcast([P, ins[n].shape[0]])))
        for t, n in ((bq_col, "L2_gnn_bq"), (bk_col, "L2_gnn_bk"), (bv_col, "L2_gnn_bv"),
                     (gamma_col, "L3_gnn_gamma"), (beta_col, "L3_gnn_beta")):
            SET_LOADS.append((t[:, :], ins[n].rearrange("(c p) -> p c", p=P)))

        block = ctx.enter_context(nc.Block())

        @block.sync
        def _(sp):
            def load_x(q):
                after(sp, made["ax"], q * G)
                after(sp, xb_made, q * G)
                sp.dma_start(x_in[:, :, :], x_d[bass.ds(q * G, G)].rearrange("g n d -> n g d")).then_inc(x_loaded, 16)

            def load_a(q):
                after(sp, made["at"], q * G)
                after(sp, a_summed, q)
                after(sp, a_held, q)
                sp.dma_start(a_in[:, :, :], adj_d[bass.ds(q * G, G)].rearrange("g n m -> n g m")).then_inc(a_loaded, 16)

            def store(q):
                for g in range(G):
                    sp.wait_ge(norm_made["ln4"], nth(q, g))
                    sp.dma_start(out[bass.ds(q * G + g, 1)].rearrange("g n d -> n (g d)"),
                                 y_out[:, g, :]).then_inc(out_stored[g], 16)

            load_x(0)
            load_a(0)
            with nc.allow_non_contiguous_dma(reason="vectors, once"):
                for dst, src in SET_LOADS:
                    sp.dma_start(dst, src).then_inc(set_loaded, 16)
            load_x(1)
            load_a(1)
            with sp.Fori(0, NG - 2) as it:
                load_x(it + 2)
                load_a(it + 2)
                store(it)
            store(NG - 2)
            store(NG - 1)
            for g in range(G):
                sp.wait_ge(out_stored[g], 16 * NG)

        @block.tensor
        def _(pe):
            def bank(first, s):
                return ps[:, first[s], :]

            def ax(q, g, o):
                if g == 0:
                    pe.wait_ge(x_loaded, q * 16 + 16)
                pe.wait_ge(read["at"], nth(q, g))
                for c in range(C):
                    m = pe.matmul(o[:, c * P:(c + 1) * P], x_in[:, g, c * P:(c + 1) * P], aT[:, g, :], start=True, stop=True)
                return m

            def at(q, g, o):
                if g == 0:
                    pe.wait_ge(a_loaded, q * 16 + 16)
                return pe.transpose(o[:, 0:P], a_in[:, g, :], ident[:, :])

            def rows(o, left, right, chunks):
                for c in range(chunks):
                    m = pe.matmul(o, left(c), right(c), start=(c == 0), stop=(c == chunks - 1))
                return m

            def h0(q, g, o):
                pe.wait_ge(read["ax"], nth(q, g))
                return rows(o[:, 0:D], lambda c: axT[:, g % 2, c, :], lambda c: w0[:, c, :], C)

            def x1t(q, g, o):
                pe.wait_ge(norm_made["ln0"], nth(q, g))
                for c in range(C):
                    m = pe.transpose(o[:, c * P:(c + 1) * P], x1[:, g, c * P:(c + 1) * P], ident[:, :])
                return m

            def amx_(q, g, o):
                pe.wait_ge(amT_made, nth(q, g))
                pe.wait_ge(norm_made["ln0"], nth(q, g))
                return pe.matmul(o[:, 0:D], amT[:, g, :], x1[:, g, :], start=True, stop=True)

            def xg(q, g, o):
                pe.wait_ge(read["x1t"], nth(q, g))
                return rows(o[:, 0:D], lambda c: x1T[:, g, c, :], lambda c: gram[:, c, :], C)

            def wt(q, g, o):
                pe.wait_ge(wm_made, q + 1)
                return pe.transpose(o[0:G, 0:P], wm[:, :], ident[:, :])

            def pb(q, g, o):
                pe.wait_ge(p_row_made, q + 1)
                return pe.transpose(o[:, 0:P], p_row[:, :], ident[:, :])

            def v1(q, g, o):
                pe.wait_ge(read["x1t"], nth(q, g))
                return rows(o[:, 0:D], lambda c: x1T[:, g, c, :], lambda c: wv1[:, c, :], C)

            def x2t(q, g, o):
                pe.wait_ge(norm_made["ln1"], nth(q, g))
                for c in range(C):
                    m = pe.transpose(o[:, c * P:(c + 1) * P], x2[:, g, c * P:(c + 1) * P], ident[:, :])
                return m

            def project(wT, f):
                def stage(q, g, o):
                    pe.wait_ge(read["x2t"], nth(q, G - 1))
                    return rows(o, lambda c: wT[:, c, f * P:(f + 1) * P], lambda c: x2T[:, c, :], C)
                return stage

            def v2_(q, g, o):
                pe.wait_ge(read["x2t"], nth(q, g))
                return rows(o[:, 0:D], lambda c: x2T[:, c, g * P:(g + 1) * P], lambda c: wvT[:, c, :], C)

            def mp_(q, g, o):
                pe.wait_ge(hb_made, nth(q, g))
                return pe.matmul(o[:, 0:P + 2], hT[:, g, :], hb[:, g, :], start=True, stop=True)

            def sc(q, g, o, b):
                if g == 0:
                    for s in ("q0", "q1", "k0", "k1"):
                        pe.wait_ge(read[s], q + 1)
                for r in range(RG):
                    for c in range(C):
                        at_ = slice(r * HD, (r + 1) * HD)
                        m = pe.matmul(ps[:, b + r, c * P:(c + 1) * P], qT[at_, c, g * P:(g + 1) * P],
                                      kT[at_, c, g * P:(g + 1) * P], start=True, stop=True)
                return m

            def pt(q, g, o, b):
                pe.wait_ge(probs_made, nth(q, g))
                for h in range(HEADS):
                    m = pe.transpose(ps[:, b + h // 4, (h % 4) * P:(h % 4 + 1) * P], z[:, g % 2, h, :], ident[:, :])
                return m

            def cx(q, g, o):
                pe.wait_ge(read["v2"], nth(q, g))
                pe.wait_ge(read["pt"], nth(q, g))
                for c in range(C):
                    for r in range(RG):
                        m = pe.matmul(o[r * HD:(r + 1) * HD, c * P:(c + 1) * P],
                                      v2[:, g, c * P + r * HD:c * P + (r + 1) * HD], pT[:, g % 2, r * C + c, :],
                                      start=True, stop=True)
                return m

            def wo(q, g, o):
                pe.wait_ge(read["cx"], nth(q, g))
                return rows(o[:, 0:D], lambda c: cT[:, g % 2, c, :], lambda c: woT[:, c, :], C)

            def tx(q, g, o):
                pe.wait_ge(norm_made["ln2"], nth(q, g))
                pe.wait_ge(read["mp"], nth(q, g))
                for c in range(C):
                    m = pe.matmul(o[:, c * P:(c + 1) * P], x3[:, g, c * P:(c + 1) * P], mp[:, g, 0:P], start=True, stop=True)
                return m

            def h1_(q, g, o):
                pe.wait_ge(read["tx"], nth(q, g))
                return rows(o, lambda c: txT[:, g % 2, c, :], lambda c: w1T[:, c, :], C)

            def mn(q, g, o):
                pe.wait_ge(norm_made["ln3"], nth(q, g))
                pe.wait_ge(read["mp"], nth(q, g))
                for c in range(C2):
                    m = pe.matmul(o[:, c * P:(c + 1) * P], hn[:, g, c * P:(c + 1) * P], mp[:, g, 0:P], start=True, stop=True)
                return m

            def y(q, g, o):
                pe.wait_ge(read["mn"], nth(q, g))
                return rows(o[:, 0:D], lambda c: mnT[:, g % 2, c, :], lambda c: w2T[:, c, :], C2)

            stages = {"at": at, "ax": ax, "h0": h0, "x1t": x1t, "amx": amx_, "xg": xg, "wt": wt, "pb": pb, "v1": v1,
                      "x2t": x2t, "q0": project(wqT, 0), "q1": project(wqT, 1), "k0": project(wkT, 0),
                      "k1": project(wkT, 1), "v2": v2_, "mp": mp_, "cx": cx, "wo": wo, "tx": tx, "h1": h1_,
                      "mn": mn, "y": y}
            wide = {"sc": sc, "pt": pt}

            def walk(schedule, it, again):
                first, before = place_banks(schedule)
                for s in schedule:
                    stage, g = s
                    if stage not in BANKS:
                        continue
                    need = {}
                    for (other, og), wrapped in before[s]:
                        if wrapped and not again:
                            continue
                        q = group_of(other, it)
                        if other in per_group:
                            v = (it if other not in FRONT else it + 1) if wrapped else q + 1
                        elif wrapped:
                            v = nth(it, og) if other in FRONT else it * G
                        else:
                            v = nth(q, og)
                        need.setdefault(other, []).append((og, wrapped, v))
                    for other, vs in need.items():
                        after(pe, read[other], max(vs, key=lambda t: (not t[1], t[0]))[2])
                    q, b = group_of(stage, it), first[s]
                    m = wide[stage](q, g, ps[:, b, :], b) if stage in wide else stages[stage](q, g, ps[:, b, :])
                    m.then_inc(made[stage], 1)

            pe.wait_ge(set_ident, 2)
            pe.wait_ge(set_loaded, 16 * len(SET_LOADS))
            for n, (_, blocks) in enumerate(TURNS):
                if n >= 8:
                    pe.wait_ge(set_read, n - 7)
                for k, blk in enumerate(blocks):
                    m = pe.transpose(ps[:, n % 8, k * P:(k + 1) * P], blk, ident[:, :])
                m.then_inc(set_made, 1)
            pe.wait_ge(set_read, NT)
            for r in range(C):
                rows(ps[:, r, 0:D], lambda c: wq1T[:, c, r * P:(r + 1) * P], lambda c: wk1T[:, c, :], C).then_inc(set_made, 1)
            pe.wait_ge(set_ready, C + C2)
            rows(ps[:, 2, 0:D], lambda c: bv_rep[:, c, :], lambda c: woT[:, c, :], C).then_inc(set_made, 1)
            rows(ps[:, 3, 0:D], lambda c: beta_rep[:, c, :], lambda c: w2T_raw[:, c, :], C2).then_inc(set_made, 1)
            pe.wait_ge(set_read, NT + 4)

            walk(FIRST["pe"], -1, False)
            for s in BANKS:
                if s in FRONT:
                    pe.wait_ge(read[s], 1 if s in per_group else G)
            walk(ORDER["pe"], 0, True)
            with pe.Fori(1, NG - 1) as it:
                walk(ORDER["pe"], it, True)
            for s in BANKS:
                k = NG if s in FRONT else NG - 1
                pe.wait_ge(read[s], k if s in per_group else k * G)
            walk(LAST["pe"], NG - 1, False)

        @block.scalar
        def _(act):
            def copy_out(stage, dst, shape=None, also=None):
                def run(q, g, o):
                    act.wait_ge(made[stage], q + 1 if stage in per_group else nth(q, g))
                    if also:
                        also(q, g)
                    d = dst(g)
                    src = o[:, 0:D] if shape is None else shape(o)
                    act.copy(d, src).then_inc(read[stage], 1)
                return run

            def pairs(o):
                return o[:, 0:C * P].rearrange("p (c n) -> p c n", c=C)

            def biased(stage, dst, bias):
                def run(q, g, o):
                    act.wait_ge(made[stage], q + 1)
                    after(act, made["sc"], q * G)
                    act.activation(dst, o, ACT.Identity, bias=bias).then_inc(read[stage], 1)
                return run

            def x1T_free(q):
                after(act, made["xg"], q * G)
                after(act, made["v1"], q * G)

            def aT_free(q):
                after(act, made["ax"], q * G)
                after(act, amT_made, q * G)
                after(act, hT_made, q)
                after(act, cnt_made, q * 2)

            def mp_free(q):
                after(act, made["tx"], q * G)
                after(act, made["mn"], q * G)
                after(act, d_made, q * 2)

            def x2T_free(q):
                after(act, made["v2"], q * G)
                for s in ("q0", "q1", "k0", "k1"):
                    after(act, made[s], q)

            def wt(q, g, o):
                act.wait_ge(p_bias_made, q + 1)
                act.activation(e_row[0:G, :], o[0:G, 0:P], ACT.Exp, bias=w_stat[0:G, 1:2], scale=INV,
                               accum_out=w_stat[0:G, 2:3]).then_inc(read["wt"], 1)

            def attn(q, g, part):
                act.wait_ge(max_made, nth(q, g))
                for h in range(part * HEADS // 2, (part + 1) * HEADS // 2):
                    m = act.activation(z[:, g % 2, h, :], z[:, g % 2, h, :], ACT.Exp, bias=z_max[:, g % 2, h:h + 1],
                                       accum_out=z_sum[:, g % 2, h:h + 1])
                m.then_inc((exp0_made, exp1_made)[part], 1)

            def pt(q, g, o, b):
                act.wait_ge(made["pt"], nth(q, g))
                after(act, made["cx"], earlier(q, g, 2))
                act.copy(pT[:, g % 2, :, :].rearrange("p (b h) n -> p b (h n)", b=2), ps[:, b:b + 2, :]).then_inc(read["pt"], 1)

            def relu(q, g, o):
                act.wait_ge(read["h1"], nth(q, g))
                after(act, norm_made["ln3"], earlier(q, g, 3))
                act.activation(hr[:, g % 3, :], h1[:, g % 2, :], ACT.Relu).then_inc(relu_made, 1)

            stages = {
                "at": copy_out("at", lambda g: aT[:, g, :], lambda o: o[:, 0:P],
                               lambda q, g: aT_free(q)),
                "ax": copy_out("ax", lambda g: axT[:, g % 2, :, :], pairs,
                               lambda q, g: after(act, made["h0"], earlier(q, g, 2))),
                "x1t": copy_out("x1t", lambda g: x1T[:, g, :, :], pairs, lambda q, g: x1T_free(q)),
                "amx": copy_out("amx", lambda g: amx[:, g % 2, :], None,
                                lambda q, g: after(act, read["xg"], earlier(q, g, 2))),
                "x2t": copy_out("x2t", lambda g: x2T[:, :, g * P:(g + 1) * P], pairs, lambda q, g: x2T_free(q)),
                "q0": biased("q0", qT[:, 0, :], bq_col[:, 0:1]), "q1": biased("q1", qT[:, 1, :], bq_col[:, 1:2]),
                "k0": biased("k0", kT[:, 0, :], bk_col[:, 0:1]), "k1": biased("k1", kT[:, 1, :], bk_col[:, 1:2]),
                "v2": copy_out("v2", lambda g: v2[:, g, :], None, lambda q, g: after(act, made["cx"], q * G)),
                "mp": copy_out("mp", lambda g: mp[:, g, :], lambda o: o[:, 0:P + 2],
                               lambda q, g: mp_free(q)),
                "cx": copy_out("cx", lambda g: cT[:, g % 2, :, :], pairs,
                               lambda q, g: after(act, made["wo"], earlier(q, g, 2))),
                "tx": copy_out("tx", lambda g: txT[:, g % 2, :, :], pairs,
                               lambda q, g: after(act, made["h1"], earlier(q, g, 2))),
                "relu": relu,
                "mn": copy_out("mn", lambda g: mnT[:, g % 2, :, :], lambda o: o.rearrange("p (c n) -> p c n", c=C2),
                               lambda q, g: after(act, made["y"], earlier(q, g, 2))),
            }

            def walk(schedule, it, products):
                first, _ = place_banks(products)
                for s in schedule:
                    stage, g = s
                    q = group_of(stage, it)
                    if stage == "pt":
                        pt(q, g, None, first[s])
                    elif stage in ("exp0", "exp1"):
                        attn(q, g, int(stage[-1]))
                    elif stage == "wexp":
                        wt(q, g, ps[:, first["wt", 0], :])
                    elif stage in stages:
                        stages[stage](q, g, ps[:, first[s], :] if s in first else None)

            walk(FIRST["act"], -1, FIRST["pe"])
            walk(ORDER["act"], 0, ORDER["pe"])
            with act.Fori(1, NG - 1) as it:
                walk(ORDER["act"], it, ORDER["pe"])
            walk(LAST["act"], NG - 1, LAST["pe"])

        @block.gpsimd
        def _(pool):
            def root(n):
                def run(q, g):
                    pool.wait_ge(aggr_made[n], nth(q, g))
                    pool.tensor_tensor(ve[n][:, g:g + 1], mv[n][:, g, 1:2], eps_col[:, :], ALU.add).then_inc(eps_made[n], 1)
                    pool.wait_ge(eps_made[n], nth(q, g))
                    pool.tensor_tensor(rs[n][:, g:g + 1], ve[n][:, g:g + 1], minus_half[:, :], ALU.pow).then_inc(root_made[n], 1)
                return run

            def xb_(q, g):
                if g == 0:
                    pool.wait_ge(x_loaded, q * 16 + 16)
                after(pool, read["h0"], q * G)
                pool.tensor_tensor(xb[:, g, :], x_in[:, g, :], b0_all[:, :], ALU.add).then_inc(xb_made, 1)

            def x2c_(q, g):
                pool.wait_ge(norm_made["ln1"], nth(q, g))
                after(pool, read["wo"], q * G)
                pool.tensor_tensor(x2c[:, g, :], x2[:, g, :], c2_all[:, :], ALU.add).then_inc(x2c_made, 1)

            def probs(q, g):
                zg = z[:, g % 2, :, :]
                pool.wait_ge(rcp_made, nth(q, g))
                pool.tensor_tensor(zg, zg, z_rcp[:, g % 2, :].unsqueeze(2).to_broadcast([P, HEADS, P]), ALU.mult)\
                    .then_inc(probs_made, 1)

            def x3b_(q, g):
                pool.wait_ge(norm_made["ln2"], nth(q, g))
                after(pool, x3c_made, q * G)
                pool.tensor_tensor(x3b[:, g, :], x3[:, g, :], b2_all[:, :], ALU.add).then_inc(x3b_half, 1)
                pool.wait_ge(x3b_half, nth(q, g))
                pool.tensor_tensor(x3b[:, g, :], x3b[:, g, :], x3[:, g, :], ALU.add).then_inc(x3b_made, 1)

            stages = {"xb": xb_, "x2c": x2c_, "probs": probs, "x3b": x3b_}
            for n in ("ln0", "ln1", "ln2", "ln3", "ln4"):
                stages[f"{n}_root"] = root(n)

            def walk(schedule, it, products):
                for stage, g in schedule:
                    if stage in stages:
                        stages[stage](group_of(stage, it), g)

            pool.memset(ones[:, :], 1.0).then_inc(set_ident, 1)
            pool.wait_ge(set_ident, 1)
            pool.affine_select(out=ident[:, :], in_=ones[:, :], compare_op=ALU.is_equal, fill=0.0, base=0,
                               pattern=[[-1, P]], channel_multiplier=1).then_inc(set_ident, 1)
            pool.wait_ge(set_loaded, 16 * len(SET_LOADS))
            pool.wait_ge(set_read, NT + 4)
            walk(FIRST["pool"], -1, FIRST["pe"])
            walk(ORDER["pool"], 0, ORDER["pe"])
            with pool.Fori(1, NG - 1) as it:
                walk(ORDER["pool"], it, ORDER["pe"])
            walk(LAST["pool"], NG - 1, LAST["pe"])

        @block.vector
        def _(dve):
            def norm(n, src, width, dst, free):
                def stats(q, g):
                    if n == "ln3":
                        dve.wait_ge(relu_made, nth(q, g))
                    else:
                        dve.wait_ge(read[src_stage[n]], nth(q, g))
                    dve.bn_stats(st[n][:, g, :], src(g)).then_inc(stats_made[n], 1)

                def aggr(q, g):
                    dve.wait_ge(set_ident, 1)
                    dve.wait_ge(stats_made[n], nth(q, g))
                    dve.bn_aggr(mv[n][:, g, :], st[n][:, g, :]).then_inc(aggr_made[n], 1)

                def scale(q, g):
                    dve.wait_ge(root_made[n], nth(q, g))
                    free(q, g)
                    dve.tensor_scalar(dst(g), src(g), mv[n][:, g, 0:1], rs[n][:, g:g + 1],
                                      ALU.subtract, ALU.mult).then_inc(norm_made[n], 1)

                return {f"{n}_stats": stats, f"{n}_aggr": aggr, f"{n}_norm": scale}

            src_stage = {"ln0": "h0", "ln1": "v1", "ln2": "wo", "ln4": "y"}

            def asum(q, g, o):
                dve.wait_ge(a_loaded, q * 16 + 16)
                after(dve, wm_made, q)
                dve.tensor_copy(mask[:, :], maskT[:, bass.ds(q * G, G)]).then_inc(mask_made, 1)
                dve.tensor_reduce(a_sum[:, :], a_in[:, :, :], AX.X, ALU.add).then_inc(a_summed, 1)
                after(dve, read["h0"], q * G)
                dve.wait_ge(a_summed, q + 1)
                dve.reciprocal(a_rsum[:, :], a_sum[:, :]).then_inc(a_rsum_made, 1)

            def am(q, g, o):
                dve.wait_ge(read["at"], nth(q, g))
                dve.wait_ge(mask_made, q + 1)
                dve.tensor_scalar(amT[:, g, :], aT[:, g, :], mask[:, g:g + 1], None, ALU.mult).then_inc(amT_made, 1)

            def h0(q, g, o):
                dve.wait_ge(made["h0"], nth(q, g))
                dve.wait_ge(xb_made, nth(q, g))
                dve.wait_ge(a_rsum_made, q + 1)
                dve.scalar_tensor_tensor(out=r0[:, g, :], in0=o[:, 0:D], scalar=a_rsum[:, g:g + 1], in1=xb[:, g, :],
                                         op0=ALU.mult, op1=ALU.add).then_inc(read["h0"], 1)

            def xg(q, g, o):
                dve.wait_ge(made["xg"], nth(q, g))
                dve.wait_ge(read["amx"], nth(q, g))
                dve.tensor_tensor_reduce(junk[:, g % 2, :], o[:, 0:D], amx[:, g % 2, :], 1.0, 0.0, ALU.mult, ALU.add,
                                         w[:, g:g + 1]).then_inc(read["xg"], 1)

            def wm_(q, g, o):
                dve.wait_ge(read["xg"], nth(q, G - 1))
                dve.tensor_tensor(wm[:, :], w[:, :], mask[:, :], ALU.mult).then_inc(wm_made, 1)

            def wmax(q, g, o):
                dve.wait_ge(made["wt"], q + 1)
                dve.tensor_reduce(w_stat[0:G, 0:1], ps[0:G, wt_bank[0], 0:P], AX.X, ALU.max).then_inc(p_max_made, 1)
                dve.wait_ge(p_max_made, q + 1)
                dve.tensor_scalar(w_stat[0:G, 1:2], w_stat[0:G, 0:1], -INV, None, ALU.mult).then_inc(p_bias_made, 1)

            def wnorm(q, g, o):
                dve.wait_ge(read["wt"], q + 1)
                dve.reciprocal(w_stat[0:G, 3:4], w_stat[0:G, 2:3]).then_inc(p_rcp_made, 1)
                dve.wait_ge(p_rcp_made, q + 1)
                dve.tensor_scalar(p_row[0:G, :], e_row[0:G, :], w_stat[0:G, 3:4], None, ALU.mult).then_inc(p_row_made, 1)

            def pcol(q, g, o):
                dve.wait_ge(made["pb"], q + 1)
                dve.tensor_copy(p_col[:, :], ps[:, pb_bank[0], 0:G]).then_inc(read["pb"], 1)

            def v1(q, g, o):
                dve.wait_ge(made["v1"], nth(q, g))
                dve.wait_ge(read["pb"], q + 1)
                dve.scalar_tensor_tensor(out=r1[:, g, :], in0=o[:, 0:D], scalar=p_col[:, g:g + 1], in1=x1[:, g, :],
                                         op0=ALU.mult, op1=ALU.add).then_inc(read["v1"], 1)

            def hyper(q, g, o):
                after(dve, made["mp"], q * G)
                dve.tensor_copy(hb[:, :, P:P + 1], aT[:, :, 0:1]).then_inc(cnt_made, 1)
                dve.tensor_scalar(hT[:, :, :], aT[:, :, :], 0.0, None, ALU.not_equal).then_inc(hT_made, 1)
                dve.wait_ge(hT_made, q + 1)
                dve.tensor_reduce(e_cnt[:, :], hT[:, :, :], AX.X, ALU.add).then_inc(cnt_made, 1)
                dve.wait_ge(cnt_made, q * 2 + 2)
                dve.tensor_scalar(e_max[:, :], e_cnt[:, :], 1.0, None, ALU.max).then_inc(emax_made, 1)
                dve.wait_ge(emax_made, q + 1)
                dve.reciprocal(e_rcp[:, :], e_max[:, :]).then_inc(ercp_made, 1)
                dve.wait_ge(ercp_made, q + 1)
                for k in range(G):
                    dve.tensor_scalar(hb[:, k, 0:P], hT[:, k, :], e_rcp[:, k:k + 1], None, ALU.mult).then_inc(hb_made, 1)

            def dinv(q, g, o):
                dve.wait_ge(read["mp"], nth(q, G - 1))
                after(dve, x3c_made, q * G)
                dsum, cnt = mp[:, :, P], mp[:, :, P + 1]
                dve.tensor_scalar(d_max[:, :], dsum, TINY, None, ALU.max).then_inc(d_step, 1)
                dve.wait_ge(d_step, q * 2 + 1)
                dve.reciprocal(d_rcp[:, :], d_max[:, :]).then_inc(d_step, 1)
                dve.wait_ge(d_step, q * 2 + 2)
                dve.scalar_tensor_tensor(out=d_inv[:, :], in0=dsum, scalar=0.0, in1=d_rcp[:, :],
                                         op0=ALU.is_gt, op1=ALU.mult).then_inc(d_made, 1)
                dve.wait_ge(d_made, q * 2 + 1)
                dve.tensor_tensor(d_cnt[:, :], d_inv[:, :], cnt, ALU.mult).then_inc(d_made, 1)

            def sc(q, g, o, b):
                dve.wait_ge(made["sc"], nth(q, g))
                dve.wait_ge(a_held, q + 1)
                after(dve, made["pt"], earlier(q, g, 2))
                zg = z[:, g % 2, :, :]
                for c in range(C):
                    m = dve.scalar_tensor_tensor(out=zg.rearrange("p (r c) n -> p r c n", c=C)[:, :, c, :],
                                                 in0=ps[:, b:b + RG, c * P:(c + 1) * P], scalar=HC,
                                                 in1=a_hold[:, g, :].unsqueeze(1).to_broadcast([P, RG, P]),
                                                 op0=ALU.mult, op1=ALU.mult)
                m.then_inc(read["sc"], 1)

            def zmax(q, g, o):
                dve.wait_ge(read["sc"], nth(q, g))
                dve.tensor_reduce(z_max[:, g % 2, :], z[:, g % 2, :, :], AX.X, ALU.max, negate=True).then_inc(max_made, 1)

            def zrcp(q, g, o):
                dve.wait_ge(exp0_made, nth(q, g))
                dve.wait_ge(exp1_made, nth(q, g))
                dve.reciprocal(z_rcp[:, g % 2, :], z_sum[:, g % 2, :]).then_inc(rcp_made, 1)

            def wo(q, g, o):
                dve.wait_ge(made["wo"], nth(q, g))
                dve.wait_ge(x2c_made, nth(q, g))
                dve.tensor_tensor(r2[:, g, :], o[:, 0:D], x2c[:, g, :], ALU.add).then_inc(read["wo"], 1)

            def h1_(q, g, o):
                dve.wait_ge(made["h1"], nth(q, g))
                dve.wait_ge(d_made, q * 2 + 2)
                after(dve, relu_made, earlier(q, g, 2))
                dve.scalar_tensor_tensor(out=h1[:, g % 2, :], in0=o, scalar=d_inv[:, g:g + 1], in1=b1_all[:, :],
                                         op0=ALU.mult, op1=ALU.add).then_inc(read["h1"], 1)

            def x3c_(q, g, o):
                dve.wait_ge(x3b_made, nth(q, g))
                after(dve, read["y"], q * G)
                dve.scalar_tensor_tensor(out=x3c[:, g, :], in0=bw_all[:, :], scalar=d_cnt[:, g:g + 1], in1=x3b[:, g, :],
                                         op0=ALU.mult, op1=ALU.add).then_inc(x3c_made, 1)

            def y(q, g, o):
                dve.wait_ge(made["y"], nth(q, g))
                dve.wait_ge(x3c_made, nth(q, g))
                dve.scalar_tensor_tensor(out=r3[:, g, :], in0=o[:, 0:D], scalar=d_inv[:, g:g + 1], in1=x3c[:, g, :],
                                         op0=ALU.mult, op1=ALU.add).then_inc(read["y"], 1)

            def hold_a(q, g, o):
                dve.wait_ge(a_loaded, q * 16 + 16)
                after(dve, read["sc"], q * G)
                dve.tensor_copy(a_hold[:, :, :], a_in[:, :, :]).then_inc(a_held, 1)

            def free1(q, g):
                after(dve, made["x1t"], q * G)
                after(dve, made["amx"], q * G)
                after(dve, read["v1"], q * G)

            def free2(q, g):
                after(dve, made["x2t"], q * G)
                after(dve, x2c_made, q * G)

            def free3(q, g):
                after(dve, made["tx"], q * G)
                after(dve, x3b_made, q * G)

            stages = {"asum": asum, "am": am, "h0": h0, "xg": xg, "wm": wm_, "wmax": wmax, "wnorm": wnorm, "pcol": pcol,
                      "v1": v1, "hyper": hyper, "dinv": dinv, "zmax": zmax, "wo": wo, "h1": h1_, "x3c": x3c_, "y": y,
                      "hold": hold_a, "zrcp": zrcp}
            wt_bank, pb_bank = [0], [0]
            plain = {}
            plain.update(norm("ln0", lambda g: r0[:, g, :], D, lambda g: x1[:, g, :], free1))
            plain.update(norm("ln1", lambda g: r1[:, g, :], D, lambda g: x2[:, g, :], free2))
            plain.update(norm("ln2", lambda g: r2[:, g, :], D, lambda g: x3[:, g, :], free3))
            plain.update(norm("ln3", lambda g: hr[:, g % 3, :], D2, lambda g: hn[:, g, :],
                              lambda q, g: after(dve, made["mn"], q * G)))
            plain.update(norm("ln4", lambda g: r3[:, g, :], D, lambda g: y_out[:, g, :],
                              lambda q, g: after(dve, out_stored[g], q * 16)))

            def walk(schedule, it, products):
                first, _ = place_banks(products)
                wt_bank[0], pb_bank[0] = first.get(("wt", 0)), first.get(("pb", 0))
                for s in schedule:
                    stage, g = s
                    q = group_of(stage, it)
                    if stage == "sc":
                        sc(q, g, None, first[s])
                    elif stage in stages:
                        stages[stage](q, g, ps[:, first[s], :] if s in first else None)
                    elif stage in plain:
                        plain[stage](q, g)

            dve.memset(minus_half[:, :], -0.5)
            dve.memset(eps_col[:, :], EPS)
            dve.memset(p_row[:, :], 0.0)
            dve.memset(hb[:, :, P + 1:P + 2], 1.0)
            dve.wait_ge(set_ident, 1)
            dve.wait_ge(set_loaded, 16 * len(SET_LOADS))
            for c in range(C):
                dve.tensor_scalar(bv_rep[:, c, :], ones[:, :], bv_col[:, c:c + 1], None, ALU.mult).then_inc(set_ready, 1)
            for c in range(C2):
                dve.tensor_scalar(beta_rep[:, c, :], ones[:, :], beta_col[:, c:c + 1], None, ALU.mult).then_inc(set_ready, 1)
            for n, (dst, blocks) in enumerate(TURNS):
                dve.wait_ge(set_made, n + 1)
                dve.tensor_copy(dst, ps[:, n % 8, 0:len(blocks) * P]).then_inc(set_read, 1)
            dve.wait_ge(set_read, NT)
            for c in range(C2):
                dve.tensor_scalar(w2T[:, c, :], w2T_raw[:, c, :], gamma_col[:, c:c + 1], None, ALU.mult)
            dve.wait_ge(set_made, NT + 4)
            dve.tensor_copy(gram[:, 0, :], ps[:, 0, 0:D]).then_inc(set_read, 1)
            dve.tensor_copy(gram[:, 1, :], ps[:, 1, 0:D]).then_inc(set_read, 1)
            dve.tensor_tensor(c2_all[:, :], ps[:, 2, 0:D], bo_all[:, :], ALU.add).then_inc(set_read, 1)
            dve.tensor_copy(bw_all[:, :], ps[:, 3, 0:D]).then_inc(set_read, 1)

            walk(FIRST["dve"], -1, FIRST["pe"])
            walk(ORDER["dve"], 0, ORDER["pe"])
            with dve.Fori(1, NG - 1) as it:
                walk(ORDER["dve"], it, ORDER["pe"])
            walk(LAST["dve"], NG - 1, LAST["pe"])


_INS = ["x", "adj", "nodemask", "L0_gnn_W", "L0_gnn_b", "L1_gnn_Wqk", "L1_gnn_Wv", "L2_gnn_Wq", "L2_gnn_bq",
        "L2_gnn_Wk", "L2_gnn_bk", "L2_gnn_Wv", "L2_gnn_bv", "L2_gnn_Wo", "L2_gnn_bo", "L3_gnn_W1", "L3_gnn_b1",
        "L3_gnn_gamma", "L3_gnn_beta", "L3_gnn_W2", "L3_gnn_b2"]


def kernel(**inputs):
    import numpy as _np
    import concourse.bacc as _bacc
    from concourse import mybir as _mybir
    from concourse.bass_utils import run_bass_kernel_spmd as _run

    nc = _bacc.Bacc("TRN2", target_bir_lowering=False, num_devices=1)
    arrays, aps = {}, {}
    for name in _INS:
        a = _np.ascontiguousarray(inputs[name])
        arrays[f"in_{name}_dram"] = a
        aps[name] = nc.dram_tensor(f"in_{name}_dram", a.shape, _mybir.dt.from_np(a.dtype), kind="ExternalInput").ap()
    x = inputs["x"]
    out = nc.dram_tensor("out_0_dram", tuple(x.shape), _mybir.dt.from_np(_np.dtype(x.dtype)), kind="ExternalOutput").ap()
    build(nc, aps, out)
    r = _run(nc, [arrays], core_ids=[0])
    return r.results[0]["out_0_dram"]
```

```python
from contextlib import ExitStack

import concourse.bass as bass
from concourse import mybir

P = 128
G = 4
HEADS = 8
RG = 4
EPS = 1e-5
TINY = 1e-37

F32 = mybir.dt.float32
F32R = mybir.dt.float32r
ALU = mybir.AluOpType
ACT = mybir.ActivationFunctionType
AX = mybir.AxisListType

FRONT = {"x2t", "x2t_lo", "q0", "k0", "q1", "k1", "v2", "asum", "at", "am", "xb", "ax", "ax_lo", "x1t_lo", "h0", "ln0_stats", "ln0_aggr", "ln0_root", "ln0_norm", "x1t", "amx", "xg", "wm", "wt", "wmax", "wexp",
         "wnorm", "pb", "pcol", "v1", "ln1_stats", "ln1_aggr", "ln1_root", "ln1_norm", "hold"}
BANKS = {"at": 1, "ax": 1, "h0": 1, "x1t": 1, "amx": 1, "xg": 1, "wt": 1, "pb": 1, "v1": 1,
         "x2t": 1, "q0": 1, "q1": 1, "k0": 1, "k1": 1, "v2": 1, "mp": 1, "sc0": 2, "sc1": 2, "pt": 2,
         "cx": 1, "wo": 1, "tx": 1, "h1": 1, "mn": 1, "y": 1}


ORDER_TEXT = {
    "pe": """
        at.0 sc1.0 ax.0 at.1 at.2 sc0.0 ax.1 sc1.1 sc0.1 at.3 h0.0 h0.1 ax.2 mp.0 sc0.2 mp.1 mp.2 pt.0 h0.2 ax.3
        mp.3 cx.0 sc1.2 pt.1 wo.0 x1t.0 sc1.3 sc0.3 x1t.1 cx.1 amx.0 amx.1 h0.3 wo.1 tx.0 xg.0 x1t.2 xg.1 amx.2
        pt.2 h1.0 x1t.3 xg.2 cx.2 tx.1 amx.3 xg.3 wo.2 pt.3 wt.0 h1.1 cx.3 v1.0 v1.1 pb.0 wo.3 tx.2 v1.2 mn.0 h1.2
        v1.3 mn.1 x2t.0 tx.3 y.0 h1.3 x2t.1 y.1 mn.2 v2.0 x2t.2 v2.1 x2t.3 y.2 mn.3 k0.0 k1.0 y.3 q1.0 q0.0 v2.2
        v2.3
    """,
    "act": """
        at.0 ax.0 at.1 at.2 exp1.0 ax.1 exp0.0 at.3 exp1.1 ax.2 exp0.1 mp.0 pt.0 mp.1 ax.3 mp.2 ln0_norm.0 mp.3
        cx.0 exp0.2 pt.1 ln0_norm.1 x1t.0 exp1.2 cx.1 ln0_norm.2 x1t.1 ln2_norm.0 amx.0 amx.1 exp1.3 tx.0 x1t.2
        exp0.3 ln0_norm.3 pt.2 ln2_norm.1 x1t.3 amx.2 cx.2 relu.0 tx.1 amx.3 pt.3 wexp.0 cx.3 relu.1 ln2_norm.2
        ln3_norm.0 tx.2 ln3_norm.1 mn.0 ln1_norm.0 ln2_norm.3 relu.2 x2t.0 tx.3 mn.1 ln1_norm.1 ln3_norm.2 relu.3
        x2t.1 ln1_norm.2 mn.2 ln1_norm.3 x2t.2 v2.0 v2.1 ln3_norm.3 x2t.3 mn.3 ln4_norm.0 k0.0 k1.0 ln4_norm.1 q1.0
        ln4_norm.2 q0.0 v2.2 ln4_norm.3 v2.3
    """,
    "dve": """
        hyper.0 asum.0 sc1.0 zmax1.0 sc0.0 ax_lo.0 zmax0.0 sc1.1 ax_lo.1 zmax1.1 h0.0 zrcp.0 sc0.1 am.0 zmax0.1
        ln0_stats.0 h0.1 ln0_aggr.0 am.1 ax_lo.2 am.2 ln0_stats.1 zrcp.1 sc0.2 zmax0.2 h0.2 ln0_aggr.1 ln0_stats.2
        ax_lo.3 cx_lo.0 sc1.2 ln0_aggr.2 zmax1.2 wo.0 am.3 ln2_stats.0 sc1.3 x1t_lo.0 ln2_aggr.0 zmax1.3 sc0.3
        zrcp.2 cx_lo.1 x1t_lo.1 h0.3 zmax0.3 ln0_stats.3 ln0_aggr.3 wo.1 ln2_stats.1 tx_lo.0 ln2_aggr.1 dinv.0
        x1t_lo.2 hold.0 xg.0 x3c.0 xg.1 zrcp.3 h1.0 x1t_lo.3 xg.2 cx_lo.2 xg.3 tx_lo.1 wo.2 wm.0 ln2_stats.2
        ln3_stats.0 ln2_aggr.2 wmax.0 ln3_aggr.0 h1.1 wnorm.0 cx_lo.3 ln3_stats.1 pcol.0 ln3_aggr.1 v1.0 wo.3
        ln1_stats.0 ln1_aggr.0 tx_lo.2 ln2_stats.3 v1.1 ln2_aggr.3 ln1_stats.1 v1.2 h1.2 ln1_aggr.1 ln1_stats.2
        mn_lo.0 v1.3 ln3_stats.2 tx_lo.3 ln1_aggr.2 ln3_aggr.2 mn_lo.1 x2t_lo.0 ln1_stats.3 x3c.1 h1.3 y.0
        ln1_aggr.3 ln3_stats.3 ln3_aggr.3 x2t_lo.1 mn_lo.2 ln4_stats.0 y.1 x2t_lo.2 ln4_aggr.0 x2t_lo.3 mn_lo.3
        x3c.2 y.2 ln4_stats.1 ln4_stats.2 ln4_aggr.1 ln4_aggr.2 x3c.3 y.3 ln4_stats.3 ln4_aggr.3
    """,
    "pool": """
        xb.0 x2c.0 x2c.1 xb.1 xb.2 probs.0 ln0_root.0 probs.1 xb.3 ln0_root.1 ln0_root.2 ln2_root.0 probs.2 x3b.0
        ln0_root.3 ln2_root.1 x2c.2 probs.3 x2c.3 x3b.1 ln2_root.2 ln3_root.0 ln3_root.1 ln1_root.0 ln2_root.3
        ln1_root.1 ln3_root.2 ln1_root.2 ln1_root.3 ln3_root.3 x3b.2 x3b.3 ln4_root.0 ln4_root.1 ln4_root.2
        ln4_root.3
    """,
}
FIRST_TEXT = {
    "pe": """
        at.0 at.1 at.2 at.3 ax.0 ax.1 ax.2 h0.0 ax.3 h0.1 h0.2 h0.3 x1t.0 amx.0 x1t.1 xg.0 amx.1 x1t.2 xg.1 amx.2
        x1t.3 amx.3 xg.2 xg.3 wt.0 v1.0 v1.1 pb.0 v1.2 v1.3 x2t.0 x2t.1 v2.0 x2t.2 v2.1 x2t.3 v2.2 q0.0 q1.0 k1.0
        k0.0 v2.3
    """,
    "act": """
        at.0 at.1 at.2 ax.0 at.3 ax.1 ax.2 ax.3 ln0_norm.0 x1t.0 ln0_norm.1 amx.0 x1t.1 ln0_norm.2 ln0_norm.3 x1t.2
        amx.1 x1t.3 amx.2 amx.3 wexp.0 ln1_norm.0 ln1_norm.1 x2t.0 x2t.1 ln1_norm.2 ln1_norm.3 x2t.2 v2.0 x2t.3
        q1.0 v2.1 q0.0 v2.2 k1.0 k0.0 v2.3
    """,
    "dve": """
        asum.0 ax_lo.0 ax_lo.1 am.0 h0.0 ln0_stats.0 ax_lo.2 ln0_aggr.0 h0.1 ax_lo.3 ln0_stats.1 ln0_aggr.1 h0.2
        am.1 ln0_stats.2 ln0_aggr.2 h0.3 ln0_stats.3 x1t_lo.0 ln0_aggr.3 am.2 x1t_lo.1 am.3 xg.0 x1t_lo.2 x1t_lo.3
        xg.1 xg.2 xg.3 wm.0 wmax.0 wnorm.0 pcol.0 v1.0 ln1_stats.0 ln1_aggr.0 v1.1 ln1_stats.1 ln1_aggr.1 v1.2
        ln1_stats.2 ln1_aggr.2 v1.3 ln1_stats.3 ln1_aggr.3 hold.0 x2t_lo.0 x2t_lo.1 x2t_lo.2 x2t_lo.3
    """,
    "pool": """
        xb.0 xb.1 xb.2 xb.3 ln0_root.0 ln0_root.1 ln0_root.2 ln0_root.3 ln1_root.0 ln1_root.1 ln1_root.2 ln1_root.3
    """,
}
LAST_TEXT = {
    "pe": """
        sc1.0 sc0.0 sc0.1 sc1.1 sc1.2 sc0.2 pt.0 sc0.3 sc1.3 cx.0 pt.1 wo.0 mp.0 mp.1 mp.2 cx.1 mp.3 pt.2 wo.1 cx.2
        tx.0 pt.3 wo.2 h1.0 cx.3 tx.1 wo.3 tx.2 h1.1 h1.2 tx.3 mn.0 h1.3 mn.1 y.0 mn.2 y.1 mn.3 y.2 y.3
    """,
    "act": """
        exp1.0 exp0.0 exp1.1 exp0.1 pt.0 exp1.2 cx.0 exp0.2 pt.1 exp1.3 exp0.3 cx.1 mp.0 pt.2 mp.1 ln2_norm.0 mp.2
        cx.2 mp.3 tx.0 pt.3 ln2_norm.1 cx.3 relu.0 tx.1 ln2_norm.2 tx.2 ln3_norm.0 relu.1 ln2_norm.3 tx.3 relu.2
        mn.0 ln3_norm.1 relu.3 ln3_norm.2 mn.1 mn.2 ln3_norm.3 mn.3 ln4_norm.0 ln4_norm.1 ln4_norm.2 ln4_norm.3
    """,
    "dve": """
        sc1.0 zmax1.0 sc0.0 zmax0.0 sc1.1 sc0.1 zmax1.1 zrcp.0 zmax0.1 hyper.0 sc1.2 zrcp.1 zmax1.2 sc0.2 zmax0.2
        cx_lo.0 sc1.3 zmax1.3 zrcp.2 sc0.3 wo.0 zmax0.3 ln2_stats.0 ln2_aggr.0 zrcp.3 cx_lo.1 wo.1 ln2_stats.1
        ln2_aggr.1 cx_lo.2 tx_lo.0 dinv.0 wo.2 ln2_stats.2 ln2_aggr.2 h1.0 cx_lo.3 ln3_stats.0 tx_lo.1 ln3_aggr.0
        wo.3 ln2_stats.3 tx_lo.2 ln2_aggr.3 h1.1 h1.2 ln3_stats.1 ln3_aggr.1 tx_lo.3 ln3_stats.2 ln3_aggr.2 mn_lo.0
        h1.3 x3c.0 x3c.1 ln3_stats.3 ln3_aggr.3 mn_lo.1 y.0 ln4_stats.0 mn_lo.2 y.1 x3c.2 x3c.3 ln4_aggr.0
        ln4_stats.1 mn_lo.3 ln4_aggr.1 y.2 ln4_stats.2 ln4_aggr.2 y.3 ln4_stats.3 ln4_aggr.3
    """,
    "pool": """
        x2c.0 probs.0 x2c.1 x2c.2 probs.1 x2c.3 probs.2 ln2_root.0 probs.3 x3b.0 ln2_root.1 ln2_root.2 ln3_root.0
        ln2_root.3 x3b.1 ln3_root.1 ln3_root.2 x3b.2 ln3_root.3 x3b.3 ln4_root.0 ln4_root.1 ln4_root.2 ln4_root.3
    """,
}

HI, LO = 0, 1
PARTS = ((HI, HI), (HI, LO), (LO, HI))
SPLIT = ("ax", "x1t", "x2t", "cx", "tx", "mn")


def numbered(text):
    return [(word.split(".")[0], int(word.split(".")[1])) for word in text.split()]


ORDER, FIRST, LAST = ({engine: numbered(text) for engine, text in texts.items()}
                      for texts in (ORDER_TEXT, FIRST_TEXT, LAST_TEXT))


def place_banks(schedule, previous=()):
    def placed(steps):
        at = 0
        for s in steps:
            n = BANKS.get(s[0], 0)
            if n:
                at = 0 if at + n > 8 else at
                yield s, range(at, at + n)
                at = (at + n) % 8

    first, before, owner = {}, {}, {}
    for s, banks in placed(previous):
        owner.update({b: (s, True) for b in banks})
    for s, banks in placed(schedule):
        first[s] = banks[0]
        before[s] = [owner[b] for b in banks if b in owner]
        owner.update({b: (s, False) for b in banks})
    return first, before


def build(nc, ins, out):
    x_d, adj_d = ins["x"], ins["adj"]
    B, N, D = x_d.shape
    D2 = ins["L3_gnn_W1"].shape[0]
    NG = B // G
    C, C2 = D // P, D2 // P
    assert N == P and B == P and C == 2
    HD = D // HEADS
    HC = 2.0 * HD ** -0.5
    INV = float(D) ** -0.5

    with ExitStack() as ctx:
        def sb(name, *shape):
            return ctx.enter_context(nc.sbuf_tensor(name, [P, *shape], F32))

        def parts(name, *shape):
            return ctx.enter_context(nc.sbuf_tensor(name, [P, 2, *shape], F32R))

        def sem(name):
            return ctx.enter_context(nc.semaphore(name))

        ps = ctx.enter_context(nc.psum_tensor("ps", [P, 8, 512], F32))

        ident, ones = sb("ident", P), sb("ones", P)
        w0, wv1, gram, wqT, wkT, wvT, woT = (
            parts(n, C, D) for n in ("w0", "wv1", "gram", "wqT", "wkT", "wvT", "woT"))
        w1T, w2T = parts("w1T", C, D2), parts("w2T", C2, D)
        b0_all, c2_all, b2_all, bw_all, b1_all = (sb(n, m) for n, m in (
            ("b0_all", D), ("c2_all", D), ("b2_all", D), ("bw_all", D), ("b1_all", D2)))
        bq_col, bk_col, maskT = sb("bq_col", C), sb("bk_col", C), sb("maskT", B)
        minus_half, eps_col = sb("minus_half", 1), sb("eps_col", 1)

        x_in, a_in = sb("x_in", G, D), sb("a_in", G, P)
        aT, amT, a_hold = sb("aT", G, P), sb("amT", G, P), sb("a_hold", G, P)
        mask, a_sum, a_rsum = sb("mask", G), sb("a_sum", G), sb("a_rsum", G)
        xb, axT, x1 = sb("xb", G, D), parts("axT", 2, C, P), sb("x1", G, D)
        x1T, amx = parts("x1T", G, C, P), sb("amx", 2, D)
        w, wm, p_row, p_col = sb("w", G), sb("wm", G), sb("p_row", P), sb("p_col", G)
        e_row, w_stat = sb("e_row", P), sb("w_stat", 4)
        x2 = sb("x2", G, D)
        hT, hb, mp = sb("hT", G, P), sb("hb", G, P + 2), sb("mp", G, P + 2)
        e_cnt, e_max, e_rcp = sb("e_cnt", G), sb("e_max", G), sb("e_rcp", G)
        d_max, d_rcp, d_inv, d_cnt = (sb(n, G) for n in ("d_max", "d_rcp", "d_inv", "d_cnt"))
        x2T, x2c = parts("x2T", C, G * P), sb("x2c", G, D)
        qT, kT, v2 = sb("qT", C, G * P), sb("kT", C, G * P), sb("v2", G, D)
        z = sb("z", 2, HEADS, P)
        z_max, z_sum, z_rcp = sb("z_max", 2, HEADS), sb("z_sum", 2, HEADS), sb("z_rcp", 2, HEADS)
        pT, cT = sb("pT", 2, HEADS, P), parts("cT", 2, C, P)
        x3, x3b, y_out = sb("x3", G, D), sb("x3b", G, D), sb("y_out", G, D)
        txT, h1, mnT = parts("txT", 2, C, P), sb("h1", G, D2), parts("mnT", 2, C2, P)
        LNS = ("ln0", "ln1", "ln2", "ln3", "ln4")
        st = {n: sb(f"{n}_st", G, 6) for n in LNS}
        mv = {n: sb(f"{n}_mv", G, 2) for n in LNS}
        ve = {n: sb(f"{n}_ve", G) for n in LNS}
        rs = {n: sb(f"{n}_rs", G) for n in LNS}
        nm = {n: sb(f"{n}_nm", G) for n in LNS}

        made = {s: sem(f"{s}_made") for s in BANKS}
        read = {s: sem(f"{s}_read") for s in BANKS}
        hi_made = {s: sem(f"{s}_hi") for s in SPLIT}
        x_loaded, a_loaded = sem("x_loaded"), sem("a_loaded")
        mask_made, amT_made, a_summed, a_rsum_made, a_held = (sem(n) for n in (
            "mask_made", "amT_made", "a_summed", "a_rsum_made", "a_held"))
        xb_made, wm_made, p_max_made, p_bias_made, p_exp_made, p_rcp_made, p_row_made = (sem(n) for n in (
            "xb_made", "wm_made", "p_max_made", "p_bias_made", "p_exp_made", "p_rcp_made", "p_row_made"))
        hT_made, cnt_made, emax_made, ercp_made, hb_made = (sem(n) for n in (
            "hT_made", "cnt_made", "emax_made", "ercp_made", "hb_made"))
        d_step, d_made, x3c_made = sem("d_step"), sem("d_made"), sem("x3c_made")
        x2c_made, x3b_half, x3b_made = sem("x2c_made"), sem("x3b_half"), sem("x3b_made")
        rcp_made, probs_made = sem("rcp_made"), sem("probs_made")
        max_made, exp_made = ([sem(f"{n}{half}_made") for half in range(2)] for n in ("max", "exp"))
        relu_made = sem("relu_made")
        stats_made, aggr_made, eps_made, root_made, shift_made, norm_made = (
            {n: sem(f"{n}_{k}") for n in LNS} for k in ("stats", "aggr", "eps", "root", "shift", "norm"))
        out_stored = [sem(f"out_stored{g}") for g in range(G)]
        weight_loaded = {n: sem(f"{n}_loaded") for n in ("w2", "qk1", "o", "w1", "q", "k", "v", "mask", "w0", "wv1")}
        vectors_loaded = sem("vectors_loaded")
        set_made, set_read, set_ready, set_ident, set_half, set_scaled = (sem(n) for n in (
            "set_made", "set_read", "set_ready", "set_ident", "set_half", "set_scaled"))

        def borrow(buffer, start, *shape):
            letters = "abc"[:len(buffer.shape) - 1]
            flat = buffer[(slice(None),) * len(buffer.shape)].rearrange(f"p {' '.join(letters)} -> p ({' '.join(letters)})")
            n = 1
            for m in shape:
                n *= m
            flat = flat[:, start:start + n]
            return flat.rearrange("p (c n) -> p c n", c=shape[0]) if len(shape) == 2 else flat

        CD = C * D
        raw = {"qk1": borrow(x2, 0, C, 2 * D), "q": borrow(x3, 0, C, D), "k": borrow(x3, CD, C, D),
               "v": borrow(v2, 0, C, D), "o": borrow(v2, CD, C, D),
               "w1": borrow(h1, 0, C2, D), "w2": borrow(h1, C2 * D, C, D2),
               "w0": borrow(y_out, 0, C, D), "wv1": borrow(y_out, CD, C, D)}
        wq1T, wk1T, woT_full = borrow(x2c, 0, C, D), borrow(x2c, CD, C, D), borrow(x3b, 0, C, D)
        w2T_raw, w2T_full = borrow(z, 0, C2, D), borrow(z, C2 * D, C2, D)
        bv_rep, beta_rep = borrow(pT, 0, C, P), borrow(pT, C * P, C2, P)
        raw_mask, bo_all = borrow(pT, (C + C2) * P, N), borrow(pT, (C + C2 + 1) * P, D)
        bv_col, gamma_col, beta_col = sb("bv_col", C), sb("gamma_col", C2), sb("beta_col", C2)

        def nth(q, g):
            return q * G + (g + 1)

        def earlier(q, g, depth):
            return q * G + (g - depth + 1) if g >= depth else q * G

        def after(eng, semaphore, value):
            if not isinstance(value, int) or value > 0:
                eng.wait_ge(semaphore, value)

        def group_of(stage, it):
            return it + 1 if stage in FRONT else it

        per_group = {"wt", "pb", "q0", "q1", "k0", "k1"}

        def turned(name, rows, cols):
            return lambda r: [raw[name][:, c, r * P:(r + 1) * P] for c in range(cols)]

        TURNS = [("w2", (w2T_raw[:, r, :],), turned("w2", C2, C)(r)) for r in range(C2)]
        for r in range(C):
            TURNS.append(("qk1", (wq1T[:, r, :],), turned("qk1", C, C)(r)))
            TURNS.append(("qk1", (wk1T[:, r, :],), turned("qk1", C, C)(C + r)))
        for r in range(C):
            TURNS.append(("o", (woT_full[:, r, :],), turned("o", C, C)(r)))
        for n, t, c in (("w1", w1T, C2), ("q", wqT, C), ("k", wkT, C), ("v", wvT, C)):
            for r in range(C):
                TURNS.append((n, (t[:, HI, r, :], t[:, LO, r, :]), turned(n, C, c)(r)))
        TURNS.append(("mask", (maskT[:, :],), [raw_mask]))
        NT = len(TURNS)

        def chunked(n):
            return ins[n].rearrange("(c p) n -> p c n", p=P)

        SP_LOADS = [("w2", "L3_gnn_W2"), ("o", "L2_gnn_Wo"), ("q", "L2_gnn_Wq"), ("v", "L2_gnn_Wv")]
        ACT_LOADS = [("qk1", "L1_gnn_Wqk"), ("w1", "L3_gnn_W1"), ("k", "L2_gnn_Wk"), ("w0", "L0_gnn_W"), ("wv1", "L1_gnn_Wv")]
        VECTORS = [(t[:, 0:ins[n].shape[0]], ins[n].unsqueeze(0).to_broadcast([P, ins[n].shape[0]]))
                   for t, n in ((b0_all, "L0_gnn_b"), (bo_all, "L2_gnn_bo"), (b1_all, "L3_gnn_b1"), (b2_all, "L3_gnn_b2"))]
        VECTORS += [(t[:, :], ins[n].rearrange("(c p) -> p c", p=P))
                    for t, n in ((bq_col, "L2_gnn_bq"), (bk_col, "L2_gnn_bk"), (bv_col, "L2_gnn_bv"),
                                 (gamma_col, "L3_gnn_gamma"), (beta_col, "L3_gnn_beta"))]
        VECTORS_LOADED = 16 * len(VECTORS)

        block = ctx.enter_context(nc.Block())

        @block.sync
        def _(sp):
            def load_x(q):
                after(sp, made["ax"], q * G)
                after(sp, xb_made, q * G)
                sp.dma_start(x_in[:, :, :], x_d[bass.ds(q * G, G)].rearrange("g n d -> n g d")).then_inc(x_loaded, 16)

            def load_a(q):
                after(sp, made["at"], q * G)
                after(sp, a_summed, q)
                after(sp, a_held, q)
                sp.dma_start(a_in[:, :, :], adj_d[bass.ds(q * G, G)].rearrange("g n m -> n g m")).then_inc(a_loaded, 16)

            def store(q):
                for g in range(G):
                    sp.wait_ge(norm_made["ln4"], nth(q, g))
                    sp.dma_start(out[bass.ds(q * G + g, 1)].rearrange("g n d -> n (g d)"),
                                 y_out[:, g, :]).then_inc(out_stored[g], 16)

            with nc.allow_non_contiguous_dma(reason="vectors, once"):
                for n, name in SP_LOADS[0:2]:
                    sp.dma_start(raw[n], chunked(name)).then_inc(weight_loaded[n], 16)
                for dst, src in VECTORS:
                    sp.dma_start(dst, src).then_inc(vectors_loaded, 16)
                for n, name in SP_LOADS[2:]:
                    sp.dma_start(raw[n], chunked(name)).then_inc(weight_loaded[n], 16)
            load_x(0)
            load_x(1)
            load_a(1)
            with sp.Fori(0, NG - 2) as it:
                load_x(it + 2)
                load_a(it + 2)
                store(it)
            store(NG - 2)
            store(NG - 1)
            for g in range(G):
                sp.wait_ge(out_stored[g], 16 * NG)

        @block.tensor
        def _(pe):
            def bank(first, s):
                return ps[:, first[s], :]

            def ax(q, g, o):
                if g == 0:
                    pe.wait_ge(x_loaded, q * 16 + 16)
                pe.wait_ge(read["at"], nth(q, g))
                for c in range(C):
                    m = pe.matmul(o[:, c * P:(c + 1) * P], x_in[:, g, c * P:(c + 1) * P], aT[:, g, :], start=True, stop=True)
                return m

            def at(q, g, o):
                if g == 0:
                    pe.wait_ge(a_loaded, q * 16 + 16)
                return pe.transpose(o[:, 0:P], a_in[:, g, :], ident[:, :])

            def rows(o, left, right, chunks):
                for c in range(chunks):
                    m = pe.matmul(o, left(c), right(c), start=(c == 0), stop=(c == chunks - 1))
                return m

            def rows3(o, left, right, chunks):
                passes = [(c, i, j) for c in range(chunks) for i, j in PARTS]
                for k, (c, i, j) in enumerate(passes):
                    m = pe.matmul(o, left(i, c), right(j, c), start=(k == 0), stop=(k == len(passes) - 1))
                return m

            def h0(q, g, o):
                pe.wait_ge(read["ax"], nth(q, g))
                return rows3(o[:, 0:D], lambda i, c: axT[:, i, g % 2, c, :], lambda i, c: w0[:, i, c, :], C)

            def x1t(q, g, o):
                pe.wait_ge(norm_made["ln0"], nth(q, g))
                for c in range(C):
                    m = pe.transpose(o[:, c * P:(c + 1) * P], x1[:, g, c * P:(c + 1) * P], ident[:, :])
                return m

            def amx_(q, g, o):
                pe.wait_ge(amT_made, nth(q, g))
                pe.wait_ge(norm_made["ln0"], nth(q, g))
                return pe.matmul(o[:, 0:D], amT[:, g, :], x1[:, g, :], start=True, stop=True)

            def xg(q, g, o):
                pe.wait_ge(read["x1t"], nth(q, g))
                return rows3(o[:, 0:D], lambda i, c: x1T[:, i, g, c, :], lambda i, c: gram[:, i, c, :], C)

            def wt(q, g, o):
                pe.wait_ge(wm_made, q + 1)
                return pe.transpose(o[0:G, 0:P], wm[:, :], ident[:, :])

            def pb(q, g, o):
                pe.wait_ge(p_row_made, q + 1)
                return pe.transpose(o[:, 0:P], p_row[:, :], ident[:, :])

            def v1(q, g, o):
                pe.wait_ge(read["x1t"], nth(q, g))
                return rows3(o[:, 0:D], lambda i, c: x1T[:, i, g, c, :], lambda i, c: wv1[:, i, c, :], C)

            def x2t(q, g, o):
                pe.wait_ge(norm_made["ln1"], nth(q, g))
                for c in range(C):
                    m = pe.transpose(o[:, c * P:(c + 1) * P], x2[:, g, c * P:(c + 1) * P], ident[:, :])
                return m

            def project(wT, f):
                def stage(q, g, o):
                    pe.wait_ge(read["x2t"], nth(q, G - 1))
                    return rows3(o, lambda i, c: wT[:, i, c, f * P:(f + 1) * P], lambda i, c: x2T[:, i, c, :], C)
                return stage

            def v2_(q, g, o):
                pe.wait_ge(read["x2t"], nth(q, g))
                return rows3(o[:, 0:D], lambda i, c: x2T[:, i, c, g * P:(g + 1) * P], lambda i, c: wvT[:, i, c, :], C)

            def mp_(q, g, o):
                pe.wait_ge(hb_made, nth(q, g))
                return pe.matmul(o[:, 0:P + 2], hT[:, g, :], hb[:, g, :], start=True, stop=True)

            def sc(half):
                def stage(q, g, o, b):
                    if g == 0:
                        for s in ("q0", "q1", "k0", "k1"):
                            pe.wait_ge(read[s], q + 1)
                    for k in range(RG // 2):
                        r = half * RG // 2 + k
                        at_ = slice(r * HD, (r + 1) * HD)
                        for c in range(C):
                            m = pe.matmul(ps[:, b + k, c * P:(c + 1) * P], qT[at_, c, g * P:(g + 1) * P],
                                          kT[at_, c, g * P:(g + 1) * P], start=True, stop=True)
                    return m
                return stage

            def pt(q, g, o, b):
                pe.wait_ge(probs_made, nth(q, g))
                for h in range(HEADS):
                    m = pe.transpose(ps[:, b + h // 4, (h % 4) * P:(h % 4 + 1) * P], z[:, g % 2, h, :], ident[:, :])
                return m

            def cx(q, g, o):
                pe.wait_ge(read["v2"], nth(q, g))
                pe.wait_ge(read["pt"], nth(q, g))
                for c in range(C):
                    for r in range(RG):
                        m = pe.matmul(o[r * HD:(r + 1) * HD, c * P:(c + 1) * P],
                                      v2[:, g, c * P + r * HD:c * P + (r + 1) * HD], pT[:, g % 2, r * C + c, :],
                                      start=True, stop=True)
                return m

            def wo(q, g, o):
                pe.wait_ge(read["cx"], nth(q, g))
                return rows3(o[:, 0:D], lambda i, c: cT[:, i, g % 2, c, :], lambda i, c: woT[:, i, c, :], C)

            def tx(q, g, o):
                pe.wait_ge(norm_made["ln2"], nth(q, g))
                pe.wait_ge(read["mp"], nth(q, g))
                for c in range(C):
                    m = pe.matmul(o[:, c * P:(c + 1) * P], x3[:, g, c * P:(c + 1) * P], mp[:, g, 0:P], start=True, stop=True)
                return m

            def h1_(q, g, o):
                pe.wait_ge(read["tx"], nth(q, g))
                return rows3(o, lambda i, c: txT[:, i, g % 2, c, :], lambda i, c: w1T[:, i, c, :], C)

            def mn(q, g, o):
                pe.wait_ge(norm_made["ln3"], nth(q, g))
                pe.wait_ge(read["mp"], nth(q, g))
                for c in range(C2):
                    m = pe.matmul(o[:, c * P:(c + 1) * P], h1[:, g, c * P:(c + 1) * P], mp[:, g, 0:P], start=True, stop=True)
                return m

            def y(q, g, o):
                pe.wait_ge(read["mn"], nth(q, g))
                return rows3(o[:, 0:D], lambda i, c: mnT[:, i, g % 2, c, :], lambda i, c: w2T[:, i, c, :], C2)

            stages = {"at": at, "ax": ax, "h0": h0, "x1t": x1t, "amx": amx_, "xg": xg, "wt": wt, "pb": pb, "v1": v1,
                      "x2t": x2t, "q0": project(wqT, 0), "q1": project(wqT, 1), "k0": project(wkT, 0),
                      "k1": project(wkT, 1), "v2": v2_, "mp": mp_, "cx": cx, "wo": wo, "tx": tx, "h1": h1_,
                      "mn": mn, "y": y}
            wide = {"sc0": sc(0), "sc1": sc(1), "pt": pt}

            def walk(schedule, it, previous):
                first, before = place_banks(schedule, previous)
                for s in schedule:
                    stage, g = s
                    if stage not in BANKS:
                        continue
                    need = {}
                    for (other, og), wrapped in before[s]:
                        q = group_of(other, it)
                        if other in per_group:
                            v = (it if other not in FRONT else it + 1) if wrapped else q + 1
                        elif wrapped:
                            v = nth(it, og) if other in FRONT else it * G
                        else:
                            v = nth(q, og)
                        need.setdefault(other, []).append((og, wrapped, v))
                    for other, vs in need.items():
                        after(pe, read[other], max(vs, key=lambda t: (not t[1], t[0]))[2])
                    q, b = group_of(stage, it), first[s]
                    m = wide[stage](q, g, ps[:, b, :], b) if stage in wide else stages[stage](q, g, ps[:, b, :])
                    m.then_inc(made[stage], 1)

            pe.wait_ge(set_ident, 2)
            for n, (load, _, blocks) in enumerate(TURNS):
                pe.wait_ge(weight_loaded[load], 16)
                if n >= 8:
                    pe.wait_ge(set_read, n - 7)
                for k, blk in enumerate(blocks):
                    m = pe.transpose(ps[:, n % 8, k * P:(k + 1) * P], blk, ident[:, :])
                m.then_inc(set_made, 1)
            pe.wait_ge(set_read, NT)
            for r in range(C):
                rows(ps[:, r, 0:D], lambda c: wq1T[:, c, r * P:(r + 1) * P], lambda c: wk1T[:, c, :], C).then_inc(set_made, 1)
            pe.wait_ge(set_ready, 2)
            rows(ps[:, 2, 0:D], lambda c: bv_rep[:, c, :], lambda c: woT_full[:, c, :], C).then_inc(set_made, 1)
            rows(ps[:, 3, 0:D], lambda c: beta_rep[:, c, :], lambda c: w2T_raw[:, c, :], C2).then_inc(set_made, 1)
            pe.wait_ge(set_read, NT + 4)

            walk(FIRST["pe"], -1, ())
            walk(ORDER["pe"], 0, FIRST["pe"])
            with pe.Fori(1, NG - 1) as it:
                walk(ORDER["pe"], it, ORDER["pe"])
            walk(LAST["pe"], NG - 1, ORDER["pe"])

        @block.scalar
        def _(act):
            def copy_out(stage, dst, shape=None, also=None):
                def run(q, g, o):
                    act.wait_ge(made[stage], nth(q, g))
                    if also:
                        also(q, g)
                    d = dst(g)
                    src = o[:, 0:D] if shape is None else shape(o)
                    act.copy(d, src).then_inc((hi_made if stage in SPLIT else read)[stage], 1)
                return run

            def norm(n, src, dst, free):
                def run(q, g, o):
                    act.wait_ge(shift_made[n], nth(q, g))
                    free(q, g)
                    act.activation(dst(g), src(g), ACT.Identity, bias=nm[n][:, g:g + 1],
                                   scale=rs[n][:, g:g + 1]).then_inc(norm_made[n], 1)
                return run

            def free1(q, g):
                after(act, made["x1t"], q * G)
                after(act, made["amx"], q * G)
                after(act, norm_made["ln1"], q * G)

            def free2(q, g):
                after(act, made["x2t"], q * G)
                after(act, x2c_made, q * G)

            def free3(q, g):
                after(act, made["tx"], q * G)
                after(act, x3b_made, q * G)

            def pairs(o):
                return o[:, 0:C * P].rearrange("p (c n) -> p c n", c=C)

            def biased(stage, dst, bias):
                def run(q, g, o):
                    act.wait_ge(made[stage], q + 1)
                    after(act, made["sc0"], q * G)
                    after(act, made["sc1"], q * G)
                    act.activation(dst, o, ACT.Identity, bias=bias).then_inc(read[stage], 1)
                return run

            def x1T_free(q):
                after(act, made["xg"], q * G)
                after(act, made["v1"], q * G)

            def aT_free(q):
                after(act, made["ax"], q * G)
                after(act, amT_made, q * G)
                after(act, hT_made, q)
                after(act, cnt_made, q * 2)

            def mp_free(q):
                after(act, made["tx"], q * G)
                after(act, made["mn"], q * G)
                after(act, d_made, q * 2)

            def x2T_free(q):
                after(act, made["v2"], q * G)
                for s in ("q0", "q1", "k0", "k1"):
                    after(act, made[s], q)

            def wt(q, g, o):
                act.wait_ge(p_bias_made, q + 1)
                act.activation(e_row[0:G, :], o[0:G, 0:P], ACT.Exp, bias=w_stat[0:G, 1:2], scale=INV,
                               accum_out=w_stat[0:G, 2:3]).then_inc(read["wt"], 1)

            def attn(q, g, part):
                act.wait_ge(max_made[part], nth(q, g))
                for h in range(part * HEADS // 2, (part + 1) * HEADS // 2):
                    m = act.activation(z[:, g % 2, h, :], z[:, g % 2, h, :], ACT.Exp, bias=z_max[:, g % 2, h:h + 1],
                                       accum_out=z_sum[:, g % 2, h:h + 1])
                m.then_inc(exp_made[part], 1)

            def pt(q, g, o, b):
                act.wait_ge(made["pt"], nth(q, g))
                after(act, made["cx"], earlier(q, g, 2))
                act.copy(pT[:, g % 2, :, :].rearrange("p (b h) n -> p b (h n)", b=2), ps[:, b:b + 2, :]).then_inc(read["pt"], 1)

            def relu(q, g, o):
                act.wait_ge(read["h1"], nth(q, g))
                act.activation(h1[:, g, :], h1[:, g, :], ACT.Relu).then_inc(relu_made, 1)

            stages = {
                "at": copy_out("at", lambda g: aT[:, g, :], lambda o: o[:, 0:P],
                               lambda q, g: aT_free(q)),
                "ax": copy_out("ax", lambda g: axT[:, HI, g % 2, :, :], pairs,
                               lambda q, g: after(act, made["h0"], earlier(q, g, 2))),
                "x1t": copy_out("x1t", lambda g: x1T[:, HI, g, :, :], pairs, lambda q, g: x1T_free(q)),
                "amx": copy_out("amx", lambda g: amx[:, g % 2, :], None,
                                lambda q, g: after(act, read["xg"], earlier(q, g, 2))),
                "x2t": copy_out("x2t", lambda g: x2T[:, HI, :, g * P:(g + 1) * P], pairs, lambda q, g: x2T_free(q)),
                "q0": biased("q0", qT[:, 0, :], bq_col[:, 0:1]), "q1": biased("q1", qT[:, 1, :], bq_col[:, 1:2]),
                "k0": biased("k0", kT[:, 0, :], bk_col[:, 0:1]), "k1": biased("k1", kT[:, 1, :], bk_col[:, 1:2]),
                "v2": copy_out("v2", lambda g: v2[:, g, :], None, lambda q, g: after(act, made["cx"], q * G)),
                "mp": copy_out("mp", lambda g: mp[:, g, :], lambda o: o[:, 0:P + 2],
                               lambda q, g: mp_free(q)),
                "cx": copy_out("cx", lambda g: cT[:, HI, g % 2, :, :], pairs,
                               lambda q, g: after(act, made["wo"], earlier(q, g, 2))),
                "tx": copy_out("tx", lambda g: txT[:, HI, g % 2, :, :], pairs,
                               lambda q, g: after(act, made["h1"], earlier(q, g, 2))),
                "relu": relu,
                "ln0_norm": norm("ln0", lambda g: xb[:, g, :], lambda g: x1[:, g, :], free1),
                "ln1_norm": norm("ln1", lambda g: x1[:, g, :], lambda g: x2[:, g, :], free2),
                "ln2_norm": norm("ln2", lambda g: x2c[:, g, :], lambda g: x3[:, g, :], free3),
                "ln3_norm": norm("ln3", lambda g: h1[:, g, :], lambda g: h1[:, g, :], lambda q, g: None),
                "ln4_norm": norm("ln4", lambda g: x3b[:, g, :], lambda g: y_out[:, g, :],
                                 lambda q, g: after(act, out_stored[g], q * 16)),
                "mn": copy_out("mn", lambda g: mnT[:, HI, g % 2, :, :], lambda o: o.rearrange("p (c n) -> p c n", c=C2),
                               lambda q, g: after(act, made["y"], earlier(q, g, 2))),
            }

            def walk(schedule, it, products):
                first, _ = place_banks(products)
                for s in schedule:
                    stage, g = s
                    q = group_of(stage, it)
                    if stage == "pt":
                        pt(q, g, None, first[s])
                    elif stage in ("exp0", "exp1"):
                        attn(q, g, int(stage[-1]))
                    elif stage == "wexp":
                        wt(q, g, ps[:, first["wt", 0], :])
                    elif stage in stages:
                        stages[stage](q, g, ps[:, first[s], :] if s in first else None)

            for n, name in ACT_LOADS[0:3]:
                act.dma_start(raw[n], chunked(name)).then_inc(weight_loaded[n], 16)
            act.dma_start(raw_mask, ins["nodemask"]).then_inc(weight_loaded["mask"], 16)
            for n, name in ACT_LOADS[3:]:
                act.dma_start(raw[n], chunked(name)).then_inc(weight_loaded[n], 16)
            act.dma_start(a_in[:, :, :], adj_d[0:G].rearrange("g n m -> n g m")).then_inc(a_loaded, 16)
            for n, (_, dst, blocks) in enumerate(TURNS):
                if len(dst) == 2:
                    act.wait_ge(set_made, n + 1)
                    act.copy(dst[HI], ps[:, n % 8, 0:len(blocks) * P]).then_inc(set_half, 1)
            act.wait_ge(set_read, NT)
            act.copy(woT[:, HI, :, :], woT_full).then_inc(set_half, 1)
            act.wait_ge(set_scaled, C2)
            act.copy(w2T[:, HI, :, :], w2T_full).then_inc(set_half, 1)
            for n, dst in (("w0", w0), ("wv1", wv1)):
                act.wait_ge(weight_loaded[n], 16)
                act.copy(dst[:, HI, :, :], raw[n]).then_inc(set_half, 1)
            for c in range(C):
                act.wait_ge(set_made, NT + c + 1)
                act.copy(gram[:, HI, c, :], ps[:, c, 0:D]).then_inc(set_half, 1)

            walk(FIRST["act"], -1, FIRST["pe"])
            walk(ORDER["act"], 0, ORDER["pe"])
            with act.Fori(1, NG - 1) as it:
                walk(ORDER["act"], it, ORDER["pe"])
            walk(LAST["act"], NG - 1, LAST["pe"])

        @block.gpsimd
        def _(pool):
            def root(n):
                def run(q, g):
                    pool.wait_ge(aggr_made[n], nth(q, g))
                    pool.tensor_tensor(ve[n][:, g:g + 1], mv[n][:, g, 1:2], eps_col[:, :], ALU.add).then_inc(eps_made[n], 1)
                    pool.wait_ge(eps_made[n], nth(q, g))
                    pool.tensor_tensor(rs[n][:, g:g + 1], ve[n][:, g:g + 1], minus_half[:, :], ALU.pow).then_inc(root_made[n], 1)
                    pool.wait_ge(set_ident, 1)
                    pool.wait_ge(root_made[n], nth(q, g))
                    pool.tensor_scalar(nm[n][:, g:g + 1], mv[n][:, g, 0:1], rs[n][:, g:g + 1], -1.0,
                                       ALU.mult, ALU.mult).then_inc(shift_made[n], 1)
                return run

            def xb_(q, g):
                if g == 0:
                    pool.wait_ge(x_loaded, q * 16 + 16)
                after(pool, norm_made["ln0"], q * G)
                pool.tensor_tensor(xb[:, g, :], x_in[:, g, :], b0_all[:, :], ALU.add).then_inc(xb_made, 1)

            def x2c_(q, g):
                pool.wait_ge(norm_made["ln1"], nth(q, g))
                after(pool, norm_made["ln2"], q * G)
                pool.tensor_tensor(x2c[:, g, :], x2[:, g, :], c2_all[:, :], ALU.add).then_inc(x2c_made, 1)

            def probs(q, g):
                zg = z[:, g % 2, :, :]
                pool.wait_ge(rcp_made, nth(q, g))
                pool.tensor_tensor(zg, zg, z_rcp[:, g % 2, :].unsqueeze(2).to_broadcast([P, HEADS, P]), ALU.mult)\
                    .then_inc(probs_made, 1)

            def x3b_(q, g):
                pool.wait_ge(norm_made["ln2"], nth(q, g))
                after(pool, norm_made["ln4"], q * G)
                pool.tensor_tensor(x3b[:, g, :], x3[:, g, :], b2_all[:, :], ALU.add).then_inc(x3b_half, 1)
                pool.wait_ge(x3b_half, nth(q, g))
                pool.tensor_tensor(x3b[:, g, :], x3b[:, g, :], x3[:, g, :], ALU.add).then_inc(x3b_made, 1)

            stages = {"xb": xb_, "x2c": x2c_, "probs": probs, "x3b": x3b_}
            for n in ("ln0", "ln1", "ln2", "ln3", "ln4"):
                stages[f"{n}_root"] = root(n)

            def walk(schedule, it, products):
                for stage, g in schedule:
                    if stage in stages:
                        stages[stage](group_of(stage, it), g)

            pool.memset(ones[:, :], 1.0).then_inc(set_ident, 1)
            pool.wait_ge(set_ident, 1)
            pool.affine_select(out=ident[:, :], in_=ones[:, :], compare_op=ALU.is_equal, fill=0.0, base=0,
                               pattern=[[-1, P]], channel_multiplier=1).then_inc(set_ident, 1)
            pool.wait_ge(vectors_loaded, VECTORS_LOADED)
            for rep, col, n in ((bv_rep, bv_col, C), (beta_rep, beta_col, C2)):
                pool.tensor_tensor(rep, ones[:, :].unsqueeze(1).to_broadcast([P, n, P]),
                                   col[:, :].unsqueeze(2).to_broadcast([P, n, P]), ALU.mult).then_inc(set_ready, 1)
            pool.wait_ge(set_read, NT + 4)
            walk(FIRST["pool"], -1, FIRST["pe"])
            walk(ORDER["pool"], 0, ORDER["pe"])
            with pool.Fori(1, NG - 1) as it:
                walk(ORDER["pool"], it, ORDER["pe"])
            walk(LAST["pool"], NG - 1, LAST["pe"])

        @block.vector
        def _(dve):
            def norm(n, src):
                def stats(q, g):
                    if n == "ln3":
                        dve.wait_ge(relu_made, nth(q, g))
                    else:
                        dve.wait_ge(read[src_stage[n]], nth(q, g))
                    dve.bn_stats(st[n][:, g, :], src(g)).then_inc(stats_made[n], 1)

                def aggr(q, g):
                    dve.wait_ge(set_ident, 1)
                    dve.wait_ge(stats_made[n], nth(q, g))
                    dve.bn_aggr(mv[n][:, g, :], st[n][:, g, :]).then_inc(aggr_made[n], 1)

                return {f"{n}_stats": stats, f"{n}_aggr": aggr}

            def low(stage, dst, shape=None):
                def run(q, g, o):
                    dve.wait_ge(hi_made[stage], nth(q, g))
                    src = o.rearrange("p (c n) -> p c n", n=P)
                    hi, lo = dst(HI, g), dst(LO, g)
                    dve.tensor_tensor(lo, src[:, 0:lo.shape[1], :], hi.bitcast(F32), ALU.subtract).then_inc(read[stage], 1)
                return run

            src_stage = {"ln0": "h0", "ln1": "v1", "ln2": "wo", "ln4": "y"}

            def asum(q, g, o):
                dve.wait_ge(a_loaded, q * 16 + 16)
                after(dve, wm_made, q)
                dve.tensor_copy(mask[:, :], maskT[:, bass.ds(q * G, G)]).then_inc(mask_made, 1)
                dve.tensor_reduce(a_sum[:, :], a_in[:, :, :], AX.X, ALU.add).then_inc(a_summed, 1)
                after(dve, read["h0"], q * G)
                dve.wait_ge(a_summed, q + 1)
                dve.reciprocal(a_rsum[:, :], a_sum[:, :]).then_inc(a_rsum_made, 1)

            def am(q, g, o):
                dve.wait_ge(read["at"], nth(q, g))
                dve.wait_ge(mask_made, q + 1)
                dve.tensor_scalar(amT[:, g, :], aT[:, g, :], mask[:, g:g + 1], None, ALU.mult).then_inc(amT_made, 1)

            def h0(q, g, o):
                dve.wait_ge(made["h0"], nth(q, g))
                dve.wait_ge(xb_made, nth(q, g))
                dve.wait_ge(a_rsum_made, q + 1)
                dve.scalar_tensor_tensor(out=xb[:, g, :], in0=o[:, 0:D], scalar=a_rsum[:, g:g + 1], in1=xb[:, g, :],
                                         op0=ALU.mult, op1=ALU.add).then_inc(read["h0"], 1)

            def xg(q, g, o):
                dve.wait_ge(made["xg"], nth(q, g))
                dve.wait_ge(read["amx"], nth(q, g))
                dve.tensor_tensor_reduce(amx[:, g % 2, :], o[:, 0:D], amx[:, g % 2, :], 1.0, 0.0, ALU.mult, ALU.add,
                                         w[:, g:g + 1]).then_inc(read["xg"], 1)

            def wm_(q, g, o):
                dve.wait_ge(read["xg"], nth(q, G - 1))
                dve.tensor_tensor(wm[:, :], w[:, :], mask[:, :], ALU.mult).then_inc(wm_made, 1)

            def wmax(q, g, o):
                dve.wait_ge(made["wt"], q + 1)
                dve.tensor_reduce(w_stat[0:G, 0:1], ps[0:G, wt_bank[0], 0:P], AX.X, ALU.max).then_inc(p_max_made, 1)
                dve.wait_ge(p_max_made, q + 1)
                dve.tensor_scalar(w_stat[0:G, 1:2], w_stat[0:G, 0:1], -INV, None, ALU.mult).then_inc(p_bias_made, 1)

            def wnorm(q, g, o):
                dve.wait_ge(read["wt"], q + 1)
                dve.reciprocal(w_stat[0:G, 3:4], w_stat[0:G, 2:3]).then_inc(p_rcp_made, 1)
                dve.wait_ge(p_rcp_made, q + 1)
                dve.tensor_scalar(p_row[0:G, :], e_row[0:G, :], w_stat[0:G, 3:4], None, ALU.mult).then_inc(p_row_made, 1)

            def pcol(q, g, o):
                dve.wait_ge(made["pb"], q + 1)
                dve.tensor_copy(p_col[:, :], ps[:, pb_bank[0], 0:G]).then_inc(read["pb"], 1)

            def v1(q, g, o):
                dve.wait_ge(made["v1"], nth(q, g))
                dve.wait_ge(read["pb"], q + 1)
                dve.scalar_tensor_tensor(out=x1[:, g, :], in0=o[:, 0:D], scalar=p_col[:, g:g + 1], in1=x1[:, g, :],
                                         op0=ALU.mult, op1=ALU.add).then_inc(read["v1"], 1)

            def hyper(q, g, o):
                after(dve, made["mp"], q * G)
                dve.tensor_copy(hb[:, :, P:P + 1], aT[:, :, 0:1]).then_inc(cnt_made, 1)
                dve.tensor_scalar(hT[:, :, :], aT[:, :, :], 0.0, None, ALU.not_equal).then_inc(hT_made, 1)
                dve.wait_ge(hT_made, q + 1)
                dve.tensor_reduce(e_cnt[:, :], hT[:, :, :], AX.X, ALU.add).then_inc(cnt_made, 1)
                dve.wait_ge(cnt_made, q * 2 + 2)
                dve.tensor_scalar(e_max[:, :], e_cnt[:, :], 1.0, None, ALU.max).then_inc(emax_made, 1)
                dve.wait_ge(emax_made, q + 1)
                dve.reciprocal(e_rcp[:, :], e_max[:, :]).then_inc(ercp_made, 1)
                dve.wait_ge(ercp_made, q + 1)
                for k in range(G):
                    dve.tensor_scalar(hb[:, k, 0:P], hT[:, k, :], e_rcp[:, k:k + 1], None, ALU.mult).then_inc(hb_made, 1)

            def dinv(q, g, o):
                dve.wait_ge(read["mp"], nth(q, G - 1))
                after(dve, x3c_made, q * G)
                dsum, cnt = mp[:, :, P], mp[:, :, P + 1]
                dve.tensor_scalar(d_max[:, :], dsum, TINY, None, ALU.max).then_inc(d_step, 1)
                dve.wait_ge(d_step, q * 2 + 1)
                dve.reciprocal(d_rcp[:, :], d_max[:, :]).then_inc(d_step, 1)
                dve.wait_ge(d_step, q * 2 + 2)
                dve.scalar_tensor_tensor(out=d_inv[:, :], in0=dsum, scalar=0.0, in1=d_rcp[:, :],
                                         op0=ALU.is_gt, op1=ALU.mult).then_inc(d_made, 1)
                dve.wait_ge(d_made, q * 2 + 1)
                dve.tensor_tensor(d_cnt[:, :], d_inv[:, :], cnt, ALU.mult).then_inc(d_made, 1)

            def sc(half):
                def run(q, g, o, b):
                    dve.wait_ge(made[f"sc{half}"], nth(q, g))
                    dve.wait_ge(a_held, q + 1)
                    after(dve, made["pt"], earlier(q, g, 2))
                    for k in range(RG // 2):
                        r = half * RG // 2 + k
                        m = dve.scalar_tensor_tensor(out=z[:, g % 2, r * C:(r + 1) * C, :],
                                                     in0=ps[:, b + k, 0:C * P].rearrange("p (c n) -> p c n", c=C),
                                                     scalar=HC, in1=a_hold[:, g, :].unsqueeze(1).to_broadcast([P, C, P]),
                                                     op0=ALU.mult, op1=ALU.mult)
                    m.then_inc(read[f"sc{half}"], 1)
                return run

            def zmax(half):
                def run(q, g, o):
                    dve.wait_ge(read[f"sc{half}"], nth(q, g))
                    hs = slice(half * HEADS // 2, (half + 1) * HEADS // 2)
                    dve.tensor_reduce(z_max[:, g % 2, hs], z[:, g % 2, hs, :], AX.X, ALU.max, negate=True)\
                        .then_inc(max_made[half], 1)
                return run

            def zrcp(q, g, o):
                for half in range(2):
                    dve.wait_ge(exp_made[half], nth(q, g))
                dve.reciprocal(z_rcp[:, g % 2, :], z_sum[:, g % 2, :]).then_inc(rcp_made, 1)

            def wo(q, g, o):
                dve.wait_ge(made["wo"], nth(q, g))
                dve.wait_ge(x2c_made, nth(q, g))
                dve.tensor_tensor(x2c[:, g, :], o[:, 0:D], x2c[:, g, :], ALU.add).then_inc(read["wo"], 1)

            def h1_(q, g, o):
                dve.wait_ge(made["h1"], nth(q, g))
                dve.wait_ge(d_made, q * 2 + 2)
                after(dve, made["mn"], q * G)
                dve.scalar_tensor_tensor(out=h1[:, g, :], in0=o, scalar=d_inv[:, g:g + 1], in1=b1_all[:, :],
                                         op0=ALU.mult, op1=ALU.add).then_inc(read["h1"], 1)

            def x3c_(q, g, o):
                dve.wait_ge(x3b_made, nth(q, g))
                dve.wait_ge(d_made, q * 2 + 2)
                dve.scalar_tensor_tensor(out=x3b[:, g, :], in0=bw_all[:, :], scalar=d_cnt[:, g:g + 1], in1=x3b[:, g, :],
                                         op0=ALU.mult, op1=ALU.add).then_inc(x3c_made, 1)

            def y(q, g, o):
                dve.wait_ge(made["y"], nth(q, g))
                dve.wait_ge(x3c_made, nth(q, g))
                dve.scalar_tensor_tensor(out=x3b[:, g, :], in0=o[:, 0:D], scalar=d_inv[:, g:g + 1], in1=x3b[:, g, :],
                                         op0=ALU.mult, op1=ALU.add).then_inc(read["y"], 1)

            def hold_a(q, g, o):
                dve.wait_ge(a_loaded, q * 16 + 16)
                after(dve, read["sc0"], q * G)
                after(dve, read["sc1"], q * G)
                dve.tensor_copy(a_hold[:, :, :], a_in[:, :, :]).then_inc(a_held, 1)

            stages = {"asum": asum, "am": am, "h0": h0, "xg": xg, "wm": wm_, "wmax": wmax, "wnorm": wnorm, "pcol": pcol,
                      "v1": v1, "hyper": hyper, "dinv": dinv, "zmax0": zmax(0), "zmax1": zmax(1), "wo": wo, "h1": h1_, "x3c": x3c_, "y": y,
                      "hold": hold_a, "zrcp": zrcp,
                      "ax_lo": low("ax", lambda i, g: axT[:, i, g % 2, :, :]),
                      "x1t_lo": low("x1t", lambda i, g: x1T[:, i, g, :, :]),
                      "x2t_lo": low("x2t", lambda i, g: x2T[:, i, :, g * P:(g + 1) * P]),
                      "cx_lo": low("cx", lambda i, g: cT[:, i, g % 2, :, :]),
                      "tx_lo": low("tx", lambda i, g: txT[:, i, g % 2, :, :]),
                      "mn_lo": low("mn", lambda i, g: mnT[:, i, g % 2, :, :])}
            wt_bank, pb_bank = [0], [0]
            plain = {}
            plain.update(norm("ln0", lambda g: xb[:, g, :]))
            plain.update(norm("ln1", lambda g: x1[:, g, :]))
            plain.update(norm("ln2", lambda g: x2c[:, g, :]))
            plain.update(norm("ln3", lambda g: h1[:, g, :]))
            plain.update(norm("ln4", lambda g: x3b[:, g, :]))

            def walk(schedule, it, products):
                first, _ = place_banks(products)
                wt_bank[0], pb_bank[0] = first.get(("wt", 0)), first.get(("pb", 0))
                for s in schedule:
                    stage, g = s
                    q = group_of(stage, it)
                    if stage in ("sc0", "sc1"):
                        sc(int(stage[-1]))(q, g, None, first[s])
                    elif stage in stages:
                        product = (stage.removesuffix("_lo"), g)
                        stages[stage](q, g, ps[:, first[product], :] if product in first else None)
                    elif stage in plain:
                        plain[stage](q, g)

            dve.memset(minus_half[:, :], -0.5)
            dve.memset(eps_col[:, :], EPS)
            dve.memset(p_row[:, :], 0.0)
            dve.memset(hb[:, :, P + 1:P + 2], 1.0)
            dve.wait_ge(set_ident, 1)
            halves = 0
            for n, (_, dst, blocks) in enumerate(TURNS):
                src = ps[:, n % 8, 0:len(blocks) * P]
                if len(dst) == 1:
                    dve.wait_ge(set_made, n + 1)
                    dve.tensor_copy(dst[0], src).then_inc(set_read, 1)
                else:
                    halves += 1
                    dve.wait_ge(set_half, halves)
                    dve.tensor_tensor(dst[LO], src, dst[HI].bitcast(F32), ALU.subtract).then_inc(set_read, 1)
            dve.wait_ge(set_read, NT)
            dve.wait_ge(vectors_loaded, VECTORS_LOADED)
            for c in range(C2):
                dve.tensor_scalar(w2T_full[:, c, :], w2T_raw[:, c, :], gamma_col[:, c:c + 1], None, ALU.mult)\
                    .then_inc(set_scaled, 1)
            for src, dst in ((woT_full, woT), (w2T_full, w2T), (raw["w0"], w0), (raw["wv1"], wv1)):
                halves += 1
                dve.wait_ge(set_half, halves)
                dve.tensor_tensor(dst[:, LO, :, :], src, dst[:, HI, :, :].bitcast(F32), ALU.subtract)
            for c in range(C):
                halves += 1
                dve.wait_ge(set_half, halves)
                dve.tensor_tensor(gram[:, LO, c, :], ps[:, c, 0:D], gram[:, HI, c, :].bitcast(F32), ALU.subtract)\
                    .then_inc(set_read, 1)
            dve.wait_ge(set_made, NT + 4)
            dve.tensor_tensor(c2_all[:, :], ps[:, 2, 0:D], bo_all, ALU.add).then_inc(set_read, 1)
            dve.tensor_copy(bw_all[:, :], ps[:, 3, 0:D]).then_inc(set_read, 1)

            walk(FIRST["dve"], -1, FIRST["pe"])
            walk(ORDER["dve"], 0, ORDER["pe"])
            with dve.Fori(1, NG - 1) as it:
                walk(ORDER["dve"], it, ORDER["pe"])
            walk(LAST["dve"], NG - 1, LAST["pe"])


_INS = ["x", "adj", "nodemask", "L0_gnn_W", "L0_gnn_b", "L1_gnn_Wqk", "L1_gnn_Wv", "L2_gnn_Wq", "L2_gnn_bq",
        "L2_gnn_Wk", "L2_gnn_bk", "L2_gnn_Wv", "L2_gnn_bv", "L2_gnn_Wo", "L2_gnn_bo", "L3_gnn_W1", "L3_gnn_b1",
        "L3_gnn_gamma", "L3_gnn_beta", "L3_gnn_W2", "L3_gnn_b2"]


def kernel(**inputs):
    import numpy as _np
    import concourse.bacc as _bacc
    from concourse import mybir as _mybir
    from concourse.bass_utils import run_bass_kernel_spmd as _run

    nc = _bacc.Bacc("TRN2", target_bir_lowering=False, num_devices=1)
    arrays, aps = {}, {}
    for name in _INS:
        a = _np.ascontiguousarray(inputs[name])
        arrays[f"in_{name}_dram"] = a
        aps[name] = nc.dram_tensor(f"in_{name}_dram", a.shape, _mybir.dt.from_np(a.dtype), kind="ExternalInput").ap()
    x = inputs["x"]
    out = nc.dram_tensor("out_0_dram", tuple(x.shape), _mybir.dt.from_np(_np.dtype(x.dtype)), kind="ExternalOutput").ap()
    build(nc, aps, out)
    r = _run(nc, [arrays], core_ids=[0])
    return r.results[0]["out_0_dram"]
```
